# Optimizing a Trainium2 kernel written in Bass

```python
import numpy as np
import jax
import jax.numpy as jnp

def _softmax(x, axis=-1):
    return jax.nn.softmax(x, axis=axis)

def _gelu(x):
    return jax.nn.gelu(x, approximate=True)

def _silu(x):
    return jax.nn.silu(x)

def _sigmoid(x):
    return jax.nn.sigmoid(x)

def _layernorm(x, axis=-1, eps=1e-05):
    m = jnp.mean(x, axis=axis, keepdims=True)
    v = jnp.var(x, axis=axis, keepdims=True)
    return (x - m) / jnp.sqrt(v + eps)

def _scatter_add(tgt, idx, src, axis=0):
    return tgt.at[idx].add(src)

def _segment_sum(src, seg, n):
    return jax.ops.segment_sum(src, seg, n)
kernel_name = 'mk_vit_tower_cls_d1_tok_img1024_r4_e984e3'

def setup_inputs(seed: int=0):
    np.random.seed(seed)
    _w = jnp.asarray

    def _rec_inputs():
        import jax
        import jax.numpy as jnp
        _rk = jax.random.key(seed)
        x = -0.00016672 + 0.999947 * jax.random.normal(jax.random.fold_in(_rk, 1), (32, 3, 96, 96), jnp.float32)
        cls_tok = 0.02 * jax.random.normal(jax.random.fold_in(_rk, 5), (1, 1, 256), jnp.float32)
        return (x, cls_tok)
    x, cls_tok = _rec_inputs()

    def _L0_tok_setup():
        import jax, jax.numpy as jnp
        import numpy as np
        P = 16

        def _patchify(x):
            B, C, H, W = x.shape
            gh, gw = (H // P, W // P)
            x = x.reshape(B, C, gh, P, gw, P)
            x = x.transpose(0, 2, 4, 1, 3, 5)
            return x.reshape(B, gh * gw, C * P * P)
        key = jax.random.key(seed)
        k1, k2, k3, k4, k5 = jax.random.split(key, 5)
        B, C, S = (64, 3, 96)
        lin_in, lout = (P * P * C, 256)
        n_patches = (S // P) ** 2
        return {'x': jax.random.normal(k1, (B, C, S, S), dtype=jnp.float32), 'W': jax.random.normal(k2, (lout, lin_in), dtype=jnp.float32) * 0.02, 'b': jax.random.normal(k3, (lout,), dtype=jnp.float32) * 0.02, 'class_token': jax.random.normal(k4, (1, 1, lout), dtype=jnp.float32) * 0.02, 'pos_embedding': jax.random.normal(k5, (1, n_patches + 1, lout), dtype=jnp.float32) * 0.02}
    _L0_tok_all = _L0_tok_setup()
    _L0_tok_in = {k: v for k, v in _L0_tok_all.items() if k in ('W', 'b', 'class_token', 'pos_embedding')}
    del _L0_tok_all

    def _L0_attn_setup():
        import jax, jax.numpy as jnp
        import numpy as np
        B, T, C = (2, 512, 256)
        LAT = 64
        N_HEAD = 16
        HEAD_DIM = C // N_HEAD
        SCALE = 1.0 / np.sqrt(HEAD_DIM).astype(np.float32)
        key = jax.random.key(seed)
        ks = jax.random.split(key, 9)
        s_in = 0.02
        return {'x': jax.random.normal(ks[0], (B, T, C), dtype=jnp.float32), 'wq_lat': jax.random.normal(ks[1], (C, LAT), dtype=jnp.float32) * s_in, 'wk_lat': jax.random.normal(ks[2], (C, LAT), dtype=jnp.float32) * s_in, 'wv_lat': jax.random.normal(ks[3], (C, LAT), dtype=jnp.float32) * s_in, 'wq_heads': jax.random.normal(ks[4], (LAT, C), dtype=jnp.float32) * s_in, 'wk_heads': jax.random.normal(ks[5], (LAT, C), dtype=jnp.float32) * s_in, 'wv_heads': jax.random.normal(ks[6], (LAT, C), dtype=jnp.float32) * s_in, 'w_proj': jax.random.normal(ks[7], (C, C), dtype=jnp.float32) * s_in, 'b_proj': jnp.zeros((C,), dtype=jnp.float32)}
    _L0_attn_all = _L0_attn_setup()
    _L0_attn_in = {k: v for k, v in _L0_attn_all.items() if k in ('wq_lat', 'wk_lat', 'wv_lat', 'wq_heads', 'wk_heads', 'wv_heads', 'w_proj', 'b_proj')}
    del _L0_attn_all

    def _L0_ffn_setup():
        import jax, jax.numpy as jnp
        import numpy as np
        D_MODEL = 256
        M = 64
        INNER = 16
        key = jax.random.key(seed)
        ks = jax.random.split(key, 9)

        def init(k, shape, fan_in):
            bound = 1.0 / np.sqrt(fan_in)
            return jax.random.uniform(k, shape, jnp.float32, -bound, bound)
        x = jax.random.normal(ks[0], (16, 1024, D_MODEL), dtype=jnp.float32)
        Win = init(ks[1], (D_MODEL, M), D_MODEL)
        bin_ = init(ks[2], (M,), D_MODEL)
        W1 = init(ks[3], (M, INNER), 1)
        b1 = init(ks[4], (M, INNER), 1)
        W2 = init(ks[5], (M, INNER), INNER)
        b2 = init(ks[6], (M,), INNER)
        Wout = init(ks[7], (M, D_MODEL), M)
        bout = init(ks[8], (D_MODEL,), M)
        return {'x': x, 'Win': Win, 'bin_': bin_, 'W1': W1, 'b1': b1, 'W2': W2, 'b2': b2, 'Wout': Wout, 'bout': bout}
    _L0_ffn_all = _L0_ffn_setup()
    _L0_ffn_in = {k: v for k, v in _L0_ffn_all.items() if k in ('Win', 'bin_', 'W1', 'b1', 'W2', 'b2', 'Wout', 'bout')}
    del _L0_ffn_all
    return {'x': x, 'cls_tok': cls_tok, 'L0_tok_W': _L0_tok_in['W'], 'L0_tok_b': _L0_tok_in['b'], 'L0_tok_class_token': _L0_tok_in['class_token'], 'L0_tok_pos_embedding': _L0_tok_in['pos_embedding'], 'L0_attn_wq_lat': _L0_attn_in['wq_lat'], 'L0_attn_wk_lat': _L0_attn_in['wk_lat'], 'L0_attn_wv_lat': _L0_attn_in['wv_lat'], 'L0_attn_wq_heads': _L0_attn_in['wq_heads'], 'L0_attn_wk_heads': _L0_attn_in['wk_heads'], 'L0_attn_wv_heads': _L0_attn_in['wv_heads'], 'L0_attn_w_proj': _L0_attn_in['w_proj'], 'L0_attn_b_proj': _L0_attn_in['b_proj'], 'L0_ffn_Win': _L0_ffn_in['Win'], 'L0_ffn_bin_': _L0_ffn_in['bin_'], 'L0_ffn_W1': _L0_ffn_in['W1'], 'L0_ffn_b1': _L0_ffn_in['b1'], 'L0_ffn_W2': _L0_ffn_in['W2'], 'L0_ffn_b2': _L0_ffn_in['b2'], 'L0_ffn_Wout': _L0_ffn_in['Wout'], 'L0_ffn_bout': _L0_ffn_in['bout']}

def reference(x, cls_tok, L0_tok_W, L0_tok_b, L0_tok_class_token, L0_tok_pos_embedding, L0_attn_wq_lat, L0_attn_wk_lat, L0_attn_wv_lat, L0_attn_wq_heads, L0_attn_wk_heads, L0_attn_wv_heads, L0_attn_w_proj, L0_attn_b_proj, L0_ffn_Win, L0_ffn_bin_, L0_ffn_W1, L0_ffn_b1, L0_ffn_W2, L0_ffn_b2, L0_ffn_Wout, L0_ffn_bout):
    import jax
    import jax.numpy as jnp

    def _L0_tok_ref(x, W, b, class_token, pos_embedding):
        import jax, jax.numpy as jnp
        import numpy as np
        P = 16

        def _patchify(x):
            B, C, H, W = x.shape
            gh, gw = (H // P, W // P)
            x = x.reshape(B, C, gh, P, gw, P)
            x = x.transpose(0, 2, 4, 1, 3, 5)
            return x.reshape(B, gh * gw, C * P * P)
        patches = _patchify(x)
        proj = jnp.einsum('bnk,dk->bnd', patches, W) + b
        B = x.shape[0]
        cls = jnp.broadcast_to(class_token, (B, 1, proj.shape[-1]))
        out = jnp.concatenate([cls, proj], axis=1) + pos_embedding
        return out

    def _L0_attn_ref(x, wq_lat, wk_lat, wv_lat, wq_heads, wk_heads, wv_heads, w_proj, b_proj):
        import jax, jax.numpy as jnp
        import numpy as np
        B, T, C = (2, 512, 256)
        LAT = 64
        N_HEAD = 16
        HEAD_DIM = C // N_HEAD
        SCALE = 1.0 / np.sqrt(HEAD_DIM).astype(np.float32)
        Bx, Tx, Cx = x.shape
        q = x @ wq_lat @ wq_heads
        k = x @ wk_lat @ wk_heads
        v = x @ wv_lat @ wv_heads
        q = q.reshape(Bx, Tx, N_HEAD, HEAD_DIM).transpose(0, 2, 1, 3)
        k = k.reshape(Bx, Tx, N_HEAD, HEAD_DIM).transpose(0, 2, 1, 3)
        v = v.reshape(Bx, Tx, N_HEAD, HEAD_DIM).transpose(0, 2, 1, 3)
        att = jnp.einsum('bhqd,bhkd->bhqk', q, k) * SCALE
        causal = jnp.tril(jnp.ones((Tx, Tx), dtype=bool))
        att = jnp.where(causal[None, None], att, -jnp.inf)
        att = jax.nn.softmax(att, axis=-1)
        y = jnp.einsum('bhqk,bhkd->bhqd', att, v)
        y = y.transpose(0, 2, 1, 3).reshape(Bx, Tx, Cx)
        return y @ w_proj + b_proj

    def _L0_ffn_ref(x, Win, bin_, W1, b1, W2, b2, Wout, bout):
        import jax, jax.numpy as jnp
        import numpy as np
        D_MODEL = 256
        M = 64
        INNER = 16
        s = jnp.einsum('btd,dm->btm', x, Win) + bin_
        h = jax.nn.relu(s[..., None] * W1 + b1)
        g = jnp.einsum('btmh,mh->btm', h, W2) + b2
        out = jnp.einsum('btm,md->btd', g, Wout) + bout
        return out
    h = _L0_tok_ref(x, L0_tok_W, L0_tok_b, L0_tok_class_token, L0_tok_pos_embedding)
    h = jnp.concatenate([jnp.broadcast_to(cls_tok, (h.shape[0], 1, h.shape[2])), h], axis=1)
    h = h + _L0_attn_ref(_layernorm(h, axis=-1), L0_attn_wq_lat, L0_attn_wk_lat, L0_attn_wv_lat, L0_attn_wq_heads, L0_attn_wk_heads, L0_attn_wv_heads, L0_attn_w_proj, L0_attn_b_proj)
    h = h + _L0_ffn_ref(_layernorm(h, axis=-1), L0_ffn_Win, L0_ffn_bin_, L0_ffn_W1, L0_ffn_b1, L0_ffn_W2, L0_ffn_b2, L0_ffn_Wout, L0_ffn_bout)
    return h

_drawn_inputs = setup_inputs


def setup_inputs(seed=0):
    import zlib

    import numpy as np

    out = dict(_drawn_inputs(seed))
    spreads = {'L0_attn_b_proj': (0.0, 0.304)}
    factors = {'cls_tok': 5.909,
     'L0_tok_class_token': 8.0,
     'L0_attn_wq_lat': 8.0,
     'L0_attn_wk_lat': 8.0,
     'L0_attn_wv_lat': 6.569,
     'L0_attn_wq_heads': 8.0,
     'L0_attn_wk_heads': 8.0,
     'L0_attn_wv_heads': 6.323,
     'L0_attn_w_proj': 6.434,
     'L0_ffn_bin_': 55.723,
     'L0_ffn_Win': 3.293,
     'L0_ffn_W1': 3.224,
     'L0_ffn_bout': 3.228}
    for name, (base, spread) in spreads.items():
        noise = np.random.default_rng([zlib.crc32(name.encode()), seed]).standard_normal(out[name].shape)
        drawn = base * np.exp(spread * noise) if base else spread * noise
        out[name] = jnp.asarray(drawn.astype(out[name].dtype))
    for name, factor in factors.items():
        out[name] = (out[name] * factor).astype(out[name].dtype)
    return out
```

```python
from contextlib import ExitStack

import concourse.bass as bass
from concourse import mybir

F32 = mybir.dt.float32
BF16 = mybir.dt.bfloat16
ALU = mybir.AluOpType
ACT = mybir.ActivationFunctionType
AX_X = mybir.AxisListType.X

IMAGES = 32
PATCH = 16
GRID = 6
NP = GRID * GRID
T = NP + 2
D = 256
DC = D // 128
KIN = 3 * PATCH * PATCH
KC = KIN // 128
LAT = 64
HEADS = 16
HD = D // HEADS
STRIPS = HEADS // 2
ROWS = 4
M = 64
INNER = 16
QB = 4
NQ = IMAGES // QB
QT = QB * T
HALF = QT // 2
S3 = 3
CH = [(0, 3), (3, 3), (6, 2)]
VW = HD + 1
EPS = 1e-5
SCALE = float(HD) ** -0.5


def build(nc, xT, wT, posT, tokb, clsT, pos0T, wq_lat, wk_lat, wv_lat, wq_heads, wk_heads, wv_heads,
          w_proj, b_proj, Win, bin_, W1, b1, W2, b2, Wout, bout, ident_c, causal_c, parity_c, block_c, out):
    with ExitStack() as ctx:
        def sb(name, shape, dt=F32):
            return ctx.enter_context(nc.sbuf_tensor(name, shape, dt))

        def ps(name, shape):
            return ctx.enter_context(nc.psum_tensor(name, shape, F32))

        def sem(name):
            return ctx.enter_context(nc.semaphore(name))

        ident = sb("ident", [128, 128])
        ident_bf = sb("ident_bf", [HALF, HALF], BF16)
        causal = sb("causal", [HALF, T])
        causal_bf = sb("causal_bf", [HALF, QB * DC, T], BF16)
        parity = sb("parity", [128, 2])
        block = sb("block", [S3 * T, STRIPS])
        w_tok = sb("w_tok", [128, KC, D])
        posb = sb("posb", [128, DC, NP])
        tok_bias = sb("tok_bias", [128, DC])
        cls2 = sb("cls2", [128, DC, 2])
        pos0 = sb("pos0", [128, DC])
        wlat = sb("wlat", [128, DC, 3 * LAT])
        wqk_heads = sb("wqk_heads", [128, D])
        wvh = sb("wvh", [LAT, D])
        wproj = sb("wproj", [128, DC, D])
        bproj = sb("bproj", [HALF, D])
        win = sb("win", [128, DC, M])
        fbin = sb("fbin", [128, 1])
        fw1 = sb("fw1", [128, INNER])
        fb1 = sb("fb1", [128, INNER])
        fw2 = sb("fw2", [128, INNER])
        fb2 = sb("fb2", [128, 1])
        neg_b1 = sb("neg_b1", [128, INNER])
        w2b1 = sb("w2b1", [128, INNER])
        gconst = sb("gconst", [128, 2])
        wout = sb("wout", [128, D])
        boutb = sb("boutb", [HALF, D])
        minus_half = sb("minus_half", [HALF, 2])

        x_sb = sb("x_sb", [128, KC, QB * NP])
        hT = sb("hT", [128, DC, QB, T])
        h = sb("h", [HALF, 2, D])
        hb = sb("hb", [HALF, 2, D])
        stats1 = sb("stats1", [HALF, 2, 6])
        mv1 = sb("mv1", [HALF, 2, 2])
        ve1 = sb("ve1", [HALF, 2])
        rstd1 = sb("rstd1", [HALF, 2])
        xn = sb("xn", [HALF, 2, D])
        xnT = sb("xnT", [128, DC, QT])
        lat_qk = sb("lat_qk", [128, QT])
        lat_v = sb("lat_v", [LAT, QB, S3, T])
        Qm = sb("Qm", [128, DC, QB, 2, T])
        Kt = sb("Kt", [128, DC, QB, T])
        Vc = sb("Vc", [S3 * T, QB, D])
        Vbd = sb("Vbd", [S3 * T, QB, STRIPS, 2, VW])
        smax = sb("smax", [HALF, ROWS, QB * DC])
        P = sb("P", [HALF, QB, STRIPS, T])
        PT = sb("PT", [S3 * T, QB, len(CH), 2 * T])
        rsum = sb("rsum", [64 + T, 2, STRIPS * 2])
        y = sb("y", [64 + T, 2, D])
        yT = sb("yT", [128, DC, QB, T])
        h2 = sb("h2", [HALF, 2, D])
        h2b = sb("h2b", [HALF, 2, D])
        stats2 = sb("stats2", [HALF, 2, 6])
        mv2 = sb("mv2", [HALF, 2, 2])
        ve2 = sb("ve2", [HALF, 2])
        rstd2 = sb("rstd2", [HALF, 2])
        xn2 = sb("xn2", [HALF, 2, D])
        xn2T = sb("xn2T", [128, DC, QT])
        s = sb("s", [128, HALF])
        hid = sb("hid", [128, INNER, HALF])
        hidw = sb("hidw", [128, INNER + 1, HALF])
        g = sb("g", [128, HALF])
        o = sb("o", [HALF, 2, D])

        bank = ps("bank", [128, 8, 512])
        scores = bank[0:HALF, 0:ROWS, 0:QB * DC * T].rearrange("p r (n k) -> p r n k", k=T)
        q_ps = bank[:, 0, 0:DC * QT]
        k_ps = bank[:, 1, 0:DC * QT]
        v_ps = [bank[0:S3 * T, 2 + i, :].rearrange("p (b d) -> p b d", b=2) for i in range(2)]
        hT_ps = bank[:, 4, 0:DC * QB * NP].rearrange("p (c n) -> p c n", c=DC)
        PT_ps = [bank[0:S3 * T, 5 + i, 0:2 * len(CH) * 2 * T].rearrange("p (b j n) -> p b j n", b=2, j=len(CH))
                 for i in range(2)]
        h_ps = bank[0:HALF, 7, :].rearrange("p (t d) -> p t d", t=2)
        y_ps = [bank[0:64 + T, 4 + t, 0:STRIPS * 2 * VW].rearrange("p (s a v) -> p s a v", s=STRIPS, a=2)
                for t in range(2)]
        xnT_ps = bank[:, 6, 0:DC * QT].rearrange("p (c n) -> p c n", c=DC)
        lqk_ps = bank[:, 7, 0:QT]
        lv_ps = bank[0:LAT, 7, QT:2 * QT].rearrange("p (b t) -> p b t", b=QB)
        yT_ps = [bank[:, 4 + u, 0:DC * 2 * T].rearrange("p (c t n) -> p c t n", c=DC, t=2) for u in range(2)]
        o_ps = [bank[0:HALF, 6 + t, 0:D] for t in range(2)]
        proj_ps = bank[0:HALF, 4, :].rearrange("p (t d) -> p t d", t=2)
        xn2T_ps = bank[:, 5, 0:DC * QT].rearrange("p (c n) -> p c n", c=DC)
        s_ps = bank[:, 6, 0:HALF]

        w_tok_in, setup_in, heads_in, proj_in, ffn_in = (
            sem("w_tok_in"), sem("setup_in"), sem("heads_in"), sem("proj_in"), sem("ffn_in"))
        x_in = sem("x_in")
        psum_clear, set_dve, set_pool = sem("psum_clear"), sem("set_dve"), sem("set_pool")
        hT_done, hT_kept = sem("hT_done"), sem("hT_kept")
        h_done, h_kept = sem("h_done"), sem("h_kept")
        st1_done, mv1_done, ve1_done, rstd1_done, xn_made = (
            sem("st1_done"), sem("mv1_done"), sem("ve1_done"), sem("rstd1_done"), sem("xn_made"))
        xnT_done, xnT_kept = sem("xnT_done"), sem("xnT_kept")
        lat_done, lat_kept = sem("lat_done"), sem("lat_kept")
        V_done, V_copied, V_kept = sem("V_done"), sem("V_copied"), sem("V_kept")
        Q_done, Q_kept = sem("Q_done"), sem("Q_kept")
        K_done, K_kept = sem("K_done"), sem("K_kept")
        S_done, max_done, sub_done, exp_done = sem("S_done"), sem("max_done"), sem("sub_done"), sem("exp_done")
        PT_done, PT_kept = sem("PT_done"), sem("PT_kept")
        y_done, rsum_done, y_made = sem("y_done"), sem("rsum_done"), sem("y_made")
        yT_done, yT_kept = sem("yT_done"), sem("yT_kept")
        proj_done, h2_made = sem("proj_done"), sem("h2_made")
        hb_made, h2b_made = sem("hb_made"), sem("h2b_made")
        st2_done, mv2_done, ve2_done, rstd2_done, xn2_made = (
            sem("st2_done"), sem("mv2_done"), sem("ve2_done"), sem("rstd2_done"), sem("xn2_made"))
        xn2T_done, xn2T_kept = sem("xn2T_done"), sem("xn2T_kept")
        s_done, s_kept = sem("s_done"), sem("s_kept")
        hid_made, hidw_made, g_made = sem("hid_made"), sem("hidw_made"), sem("g_made")
        o_done, o_made, o_out = sem("o_done"), sem("o_made"), sem("o_out")

        x_v = xT.rearrange("q p n -> q p n")
        out_v = out.rearrange("(q i) t d -> q (i t) d", i=QB).rearrange("q (a r) d -> q r a d", a=2)
        blk = ctx.enter_context(nc.Block())

        def steps(eng, step):
            step(0, first=True)
            with eng.Fori(1, NQ - 1) as i:
                step(i)
            step(NQ - 1, last=True)

        @blk.sync
        def _(sp):
            sp.dma_start(x_sb[:].rearrange("p k n -> p (k n)"), x_v[0]).then_inc(x_in, 16)
            sp.dma_start(w_tok[:], wT).then_inc(w_tok_in, 16)
            sp.dma_start(posb[:], posT).then_inc(setup_in, 16)
            sp.dma_start(tok_bias[:], tokb).then_inc(setup_in, 16)
            sp.dma_start(cls2[:], clsT).then_inc(setup_in, 16)
            sp.dma_start(pos0[:], pos0T).then_inc(setup_in, 16)
            sp.dma_start(wproj[:], w_proj.rearrange("(c p) n -> p c n", p=128)).then_inc(proj_in, 16)
            sp.dma_start(win[:], Win.rearrange("(c p) n -> p c n", p=128)).then_inc(proj_in, 16)

            def load(q):
                sp.wait_ge(hT_done, q)
                sp.dma_start(x_sb[:].rearrange("p k n -> p (k n)"),
                             x_v[bass.ds(q, 1)].rearrange("a p n -> (a p) n")).then_inc(x_in, 16)

            def store(q):
                sp.wait_ge(o_made, q + 1)
                sp.dma_start(out_v[bass.ds(q, 1)].rearrange("a r t d -> (a r) t d"), o[:]).then_inc(o_out, 16)

            def step(i, first=False, last=False):
                if not last:
                    load(i + 1)
                if not first:
                    store(i - 1)

            steps(sp, step)
            store(NQ - 1)
            sp.wait_ge(o_out, 16 * NQ)

        @blk.gpsimd
        def _(pool):
            for t in range(2):
                rows = slice(64 * t, 64 * t + 64)
                pool.dma_start(wout[rows, :], Wout).then_inc(ffn_in, 16)
                pool.dma_start(fbin[rows, :], bin_.rearrange("(m a) -> m a", a=1)).then_inc(ffn_in, 16)
                pool.dma_start(fw1[rows, :], W1).then_inc(ffn_in, 16)
                pool.dma_start(fb1[rows, :], b1).then_inc(ffn_in, 16)
                pool.dma_start(fw2[rows, :], W2).then_inc(ffn_in, 16)
                pool.dma_start(fb2[rows, :], b2.rearrange("(m a) -> m a", a=1)).then_inc(ffn_in, 16)
            pool.dma_start(bproj[:], b_proj.rearrange("(a n) -> a n", a=1).broadcast_to([HALF, D])).then_inc(ffn_in, 16)
            pool.dma_start(boutb[:], bout.rearrange("(a n) -> a n", a=1).broadcast_to([HALF, D])).then_inc(ffn_in, 16)
            pool.memset(minus_half[:], -0.5).then_inc(set_pool, 1)
            pool.memset(Vbd[:], 0.0).then_inc(set_pool, 1)
            pool.wait_ge(set_pool, 2)
            pool.wait_ge(heads_in, 16 * 7)
            for b in range(QB):
                pool.tensor_copy(Vbd[:, b, :, :, HD], block[:].unsqueeze(2).to_broadcast([S3 * T, STRIPS, 2]))\
                    .then_inc(set_pool, 1)
            pool.wait_ge(ffn_in, 16 * 14)

            def rstd(ve, r, ready, done, n):
                pool.wait_ge(ready, n + 1)
                pool.tensor_tensor(r[:], ve[:], minus_half[:], ALU.pow).then_inc(done, 1)

            def weigh_hidden(q):
                pool.wait_ge(hid_made, q + 1)
                if not isinstance(q, int) or q >= 1:
                    pool.wait_ge(g_made, q)
                pool.tensor_tensor(hidw[:, 0:INNER, :], hid[:],
                                   fw2[:].unsqueeze(2).to_broadcast([128, INNER, HALF]), ALU.mult).then_inc(hidw_made, 1)

            def spread_v(q, first_quad=False):
                if not first_quad:
                    pool.wait_ge(y_done, 2 * q)
                for i in range(2):
                    pool.wait_ge(V_copied, 2 * q + i + 1)
                    for b in (2 * i, 2 * i + 1):
                        last = pool.tensor_tensor(
                            Vbd[:, b, :, :, 0:HD], Vc[:, b, :].rearrange("p (s a d) -> p s a d", s=STRIPS, a=2),
                            block[:].unsqueeze(2).unsqueeze(3).to_broadcast([S3 * T, STRIPS, 2, HD]), ALU.mult)
                last.then_inc(V_kept, 1)

            def add_bproj(q):
                pool.wait_ge(h_kept, q + 1)
                pool.tensor_tensor(hb[:], h[:], bproj[:].unsqueeze(1).to_broadcast([HALF, 2, D]), ALU.add).then_inc(hb_made, 1)

            rstd(ve1, rstd1, ve1_done, rstd1_done, 0)
            spread_v(0, first_quad=True)
            add_bproj(0)

            def step(i, first=False, last=False):
                if not last:
                    rstd(ve1, rstd1, ve1_done, rstd1_done, i + 1)
                if not first:
                    weigh_hidden(i - 1)
                if not last:
                    spread_v(i + 1)
                rstd(ve2, rstd2, ve2_done, rstd2_done, i)
                pool.wait_ge(h2_made, i + 1)
                if not last:
                    add_bproj(i + 1)
                if not first:
                    pool.wait_ge(o_made, i)
                pool.tensor_tensor(h2b[:], h2[:], boutb[:].unsqueeze(1).to_broadcast([HALF, 2, D]), ALU.add)\
                    .then_inc(h2b_made, 1)

            steps(pool, step)
            weigh_hidden(NQ - 1)

        @blk.scalar
        def _(act):
            act.dma_start(ident[:], ident_c).then_inc(heads_in, 16)
            act.dma_start(causal[:], causal_c).then_inc(heads_in, 16)
            act.dma_start(parity[:], parity_c).then_inc(heads_in, 16)
            act.dma_start(block[:], block_c).then_inc(heads_in, 16)
            for n, w in enumerate((wq_lat, wk_lat, wv_lat)):
                act.dma_start(wlat[:, :, n * LAT:(n + 1) * LAT], w.rearrange("(c p) n -> p c n", p=128)).then_inc(w_tok_in, 16)
            act.dma_start(wqk_heads[0:LAT, :], wq_heads).then_inc(heads_in, 16)
            act.dma_start(wqk_heads[LAT:128, :], wk_heads).then_inc(heads_in, 16)
            act.dma_start(wvh[:], wv_heads).then_inc(heads_in, 16)
            act.wait_ge(heads_in, 16 * 7)
            act.wait_ge(psum_clear, 1)

            def keep_h(q):
                act.wait_ge(h_done, q + 1)
                if not isinstance(q, int) or q >= 1:
                    act.wait_ge(hb_made, q)
                    act.wait_ge(xn_made, 2 * q)
                act.activation(h[:], h_ps, ACT.Copy).then_inc(h_kept, 1)

            def keep_xnT(q):
                act.wait_ge(xnT_done, q + 1)
                act.activation(xnT[:], xnT_ps, ACT.Copy).then_inc(xnT_kept, 1)

            def keep_lat(q):
                act.wait_ge(lat_done, q + 1)
                act.activation(lat_qk[:], lqk_ps, ACT.Copy).then_inc(lat_kept, 1)
                act.activation(lat_v[:], lv_ps.unsqueeze(2).to_broadcast([LAT, QB, S3, T]), ACT.Copy).then_inc(lat_kept, 1)

            def copy_v(q):
                if not isinstance(q, int) or q >= 1:
                    act.wait_ge(V_kept, q)
                for i in range(2):
                    act.wait_ge(V_done, 2 * q + i + 1)
                    act.activation(Vc[:, 2 * i:2 * i + 2, :], v_ps[i], ACT.Copy).then_inc(V_copied, 1)

            def keep_qk(q):
                act.wait_ge(Q_done, q + 1)
                for a in range(2):
                    act.activation(Qm[:, :, :, a, :].rearrange("p c b t -> p (c b) t"),
                                   q_ps.rearrange("p (n t) -> p n t", t=T), ACT.Copy,
                                   scale=parity[:, a:a + 1]).then_inc(Q_kept, 1)
                act.wait_ge(K_done, q + 1)
                act.activation(Kt[:].rearrange("p c b t -> p (c b t)"), k_ps, ACT.Copy).then_inc(K_kept, 1)

            def exponentials(q):
                for r in range(ROWS):
                    act.wait_ge(sub_done, ROWS * q + r + 1)
                    Pr = P[:].rearrange("p b (c r) k -> p b c r k", r=ROWS)[:, :, :, r, :]
                    act.activation(Pr, Pr, ACT.Exp, scale=SCALE).then_inc(exp_done, 1)

            def keep_PT(q):
                if not isinstance(q, int) or q >= 1:
                    act.wait_ge(y_done, 2 * q)
                for i in range(2):
                    act.wait_ge(PT_done, 2 * q + i + 1)
                    act.activation(PT[:, 2 * i:2 * i + 2, :, :], PT_ps[i], ACT.Copy).then_inc(PT_kept, 1)

            def keep_yT(q):
                act.wait_ge(yT_done, q + 1)
                for u in range(2):
                    act.activation(yT[:].rearrange("p c (t u) n -> p c t u n", u=2)[:, :, :, u, :],
                                   yT_ps[u], ACT.Copy).then_inc(yT_kept, 1)

            def keep_xn2T(q):
                act.wait_ge(xn2T_done, q + 1)
                act.activation(xn2T[:], xn2T_ps, ACT.Copy).then_inc(xn2T_kept, 1)

            keep_h(0)
            keep_xnT(0)
            keep_lat(0)
            copy_v(0)
            keep_qk(0)

            def step(i, first=False, last=False):
                exponentials(i)
                keep_PT(i)
                if not last:
                    keep_h(i + 1)
                    keep_xnT(i + 1)
                    keep_lat(i + 1)
                keep_yT(i)
                if not last:
                    copy_v(i + 1)
                    keep_qk(i + 1)
                keep_xn2T(i)

            steps(act, step)

        @blk.vector
        def _(dve):
            dve.memset(bank[:], 0.0).then_inc(psum_clear, 1)
            dve.memset(rsum[:], 1.0).then_inc(set_dve, 1)
            dve.wait_ge(setup_in, 16 * 4)
            for c in range(DC):
                dve.tensor_scalar(posb[:, c, :], posb[:, c, :], tok_bias[:, c:c + 1], None, ALU.add).then_inc(set_dve, 1)
            for b in range(QB):
                dve.tensor_copy(hT[:, :, b, 0], cls2[:, :, 0]).then_inc(set_dve, 1)
                dve.tensor_tensor(hT[:, :, b, 1], cls2[:, :, 1], pos0[:], ALU.add).then_inc(set_dve, 1)
            dve.wait_ge(heads_in, 16 * 7)
            dve.tensor_copy(ident_bf[:], ident[0:HALF, 0:HALF]).then_inc(set_dve, 1)
            dve.tensor_copy(causal_bf[:], causal[:].unsqueeze(1).to_broadcast([HALF, QB * DC, T])).then_inc(set_dve, 1)
            dve.wait_ge(psum_clear, 1)
            dve.wait_ge(set_dve, 3 + 2 * QB + 2)

            def keep_hT(q):
                dve.wait_ge(hT_done, q + 1)
                if not isinstance(q, int) or q >= 1:
                    dve.wait_ge(h_done, q)
                dve.tensor_tensor(hT[:].rearrange("p c b t -> p c b t")[:, 0, :, 2:T],
                                  hT_ps[:, 0, :].rearrange("p (b n) -> p b n", b=QB),
                                  posb[:, 0, :].unsqueeze(1).to_broadcast([128, QB, NP]), ALU.add)
                dve.tensor_tensor(hT[:, 1, :, 2:T],
                                  hT_ps[:, 1, :].rearrange("p (b n) -> p b n", b=QB),
                                  posb[:, 1, :].unsqueeze(1).to_broadcast([128, QB, NP]), ALU.add).then_inc(hT_kept, 1)

            def norm(src, stats, mv, ve, r, dst, st_done, mv_done, ve_done, r_done, made, n, kept, free):
                dve.wait_ge(kept, n + 1)
                for t in range(2):
                    dve.bn_stats(stats[:, t, :], src[:, t, :]).then_inc(st_done, 1)
                dve.wait_ge(st_done, 2 * n + 2)
                dve.nop(nofuse=True)
                for t in range(2):
                    dve.bn_aggr(mv[:, t, :], stats[:, t, :]).then_inc(mv_done, 1)
                dve.wait_ge(mv_done, 2 * n + 2)
                dve.tensor_scalar(ve[:], mv[:, :, 1], EPS, None, ALU.add).then_inc(ve_done, 1)
                dve.wait_ge(r_done, n + 1)
                if not isinstance(n, int) or n >= 1:
                    dve.wait_ge(free, n)
                for t in range(2):
                    dve.tensor_scalar(dst[:, t, :], src[:, t, :], mv[:, t, 0:1], r[:, t:t + 1],
                                      ALU.subtract, ALU.mult).then_inc(made, 1)

            def norm1(q):
                norm(h, stats1, mv1, ve1, rstd1, xn, st1_done, mv1_done, ve1_done, rstd1_done, xn_made, q, h_kept, xnT_done)

            def softmax(q):
                if not isinstance(q, int) or q >= 1:
                    dve.wait_ge(PT_done, 2 * q)
                for r in range(ROWS):
                    dve.wait_ge(S_done, ROWS * q + r + 1)
                    dve.tensor_reduce(smax[:, r, :], scores[:, r, :, :], AX_X, ALU.max).then_inc(max_done, 1)
                for r in range(ROWS):
                    dve.wait_ge(max_done, ROWS * q + r + 1)
                    dve.tensor_tensor(P[:].rearrange("p b (c r) k -> p b c r k", r=ROWS)[:, :, :, r, :],
                                      scores[:, r, :, :].rearrange("p (b c) k -> p b c k", b=QB),
                                      smax[:, r, :].rearrange("p (b c) -> p b c", b=QB).unsqueeze(3)
                                      .to_broadcast([HALF, QB, DC, T]), ALU.subtract).then_inc(sub_done, 1)

            def weighted_values(q):
                for t in range(2):
                    dve.wait_ge(y_done, 2 * q + t + 1)
                    for u in range(2):
                        rows = slice(64 * u, 64 * u + T)
                        last = dve.reciprocal(rsum[rows, t, :].rearrange("p (s a) -> p s a", a=2), y_ps[t][rows, :, :, HD])
                    last.then_inc(rsum_done, 1)
                if not isinstance(q, int) or q >= 1:
                    dve.wait_ge(yT_done, q)
                for t in range(2):
                    dve.wait_ge(rsum_done, 2 * q + t + 1)
                    dve.tensor_tensor(y[:, t, :].rearrange("p (s a d) -> p s a d", s=STRIPS, a=2),
                                      y_ps[t][:, :, :, 0:HD],
                                      rsum[:, t, :].rearrange("p (s a) -> p s a", a=2).unsqueeze(3)
                                      .to_broadcast([64 + T, STRIPS, 2, HD]), ALU.mult).then_inc(y_made, 1)

            def residual_norm2(q):
                dve.wait_ge(proj_done, q + 1)
                dve.wait_ge(hb_made, q + 1)
                if not isinstance(q, int) or q >= 1:
                    dve.wait_ge(h2b_made, q)
                dve.tensor_tensor(h2[:], proj_ps, hb[:], ALU.add).then_inc(h2_made, 1)
                norm(h2, stats2, mv2, ve2, rstd2, xn2, st2_done, mv2_done, ve2_done, rstd2_done, xn2_made, q,
                     h2_made, xn2T_done)

            def hidden(q):
                dve.wait_ge(s_done, q + 1)
                dve.tensor_scalar(s[:], s_ps, fbin[:, 0:1], None, ALU.add).then_inc(s_kept, 1)
                dve.wait_ge(s_kept, q + 1)
                if not isinstance(q, int) or q >= 1:
                    dve.wait_ge(hidw_made, q)
                for k in range(INNER):
                    last = dve.tensor_scalar(hid[:, k, :], s[:], fw1[:, k:k + 1], neg_b1[:, k:k + 1], ALU.mult, ALU.max)
                last.then_inc(hid_made, 1)

            def sum_hidden(q):
                dve.wait_ge(hidw_made, q + 1)
                if not isinstance(q, int) or q >= 1:
                    dve.wait_ge(o_done, q)
                dve.tensor_reduce(g[:], hidw[:].rearrange("p k n -> p n k"), AX_X, ALU.add).then_inc(g_made, 1)

            def result(q):
                dve.wait_ge(o_done, q + 1)
                dve.wait_ge(h2b_made, q + 1)
                if not isinstance(q, int) or q >= 1:
                    dve.wait_ge(o_out, 16 * q)
                for t in range(2):
                    last = dve.tensor_tensor(o[:, t, :], o_ps[t], h2b[:, t, :], ALU.add)
                last.then_inc(o_made, 1)

            keep_hT(0)
            norm1(0)
            dve.wait_ge(ffn_in, 16 * 14)
            dve.tensor_scalar(neg_b1[:], fb1[:], -1.0, None, ALU.mult).then_inc(set_dve, 1)
            dve.tensor_tensor(w2b1[:], fw2[:], fb1[:], ALU.mult).then_inc(set_dve, 1)
            dve.wait_ge(set_dve, 3 + 2 * QB + 4)
            dve.tensor_reduce(gconst[:, 0:1], w2b1[:], AX_X, ALU.add).then_inc(set_dve, 1)
            dve.wait_ge(set_dve, 3 + 2 * QB + 5)
            dve.tensor_tensor(gconst[:, 1:2], gconst[:, 0:1], fb2[:], ALU.add).then_inc(set_dve, 1)
            dve.wait_ge(set_dve, 3 + 2 * QB + 6)
            dve.tensor_copy(hidw[:, INNER, :], gconst[:, 1:2].to_broadcast([128, HALF])).then_inc(set_dve, 1)
            dve.wait_ge(set_dve, 3 + 2 * QB + 7)

            def step(i, first=False, last=False):
                softmax(i)
                if not last:
                    keep_hT(i + 1)
                if not first:
                    hidden(i - 1)
                if not last:
                    norm1(i + 1)
                weighted_values(i)
                if not first:
                    sum_hidden(i - 1)
                    result(i - 1)
                residual_norm2(i)

            steps(dve, step)
            hidden(NQ - 1)
            sum_hidden(NQ - 1)
            result(NQ - 1)

        @blk.tensor
        def _(pe):
            mm = pe.matmul
            pe.wait_ge(heads_in, 16 * 7)
            pe.wait_ge(w_tok_in, 16 * 4)
            pe.wait_ge(psum_clear, 1)
            pe.wait_ge(set_dve, 3 + 2 * QB + 2)

            def patches(q):
                pe.wait_ge(x_in, 16 * (q + 1))
                if not isinstance(q, int) or q >= 2:
                    pe.wait_ge(h2_made, q - 1)
                for c in range(DC):
                    for k in range(KC):
                        last = mm(hT_ps[:, c, :], w_tok[:, k, c * 128:(c + 1) * 128], x_sb[:, k, :],
                                  start=(k == 0), stop=(k == KC - 1))
                last.then_inc(hT_done, 1)

            def token_major(q):
                pe.wait_ge(hT_kept, q + 1)
                for t in range(2):
                    for c in range(DC):
                        last = pe.transpose(h_ps[:, t, c * 128:(c + 1) * 128],
                                            hT[:, c, 2 * t:2 * t + 2, :].rearrange("p b t -> p (b t)"), ident[:])
                last.then_inc(h_done, 1)

            def xn_transposes(q):
                for t in range(2):
                    pe.wait_ge(xn_made, 2 * q + t + 1)
                    for c in range(DC):
                        last = pe.transpose(xnT_ps[:, c, t * HALF:(t + 1) * HALF], xn[:, t, c * 128:(c + 1) * 128],
                                            ident[0:HALF, 0:HALF])
                last.then_inc(xnT_done, 1)

            def latents(q):
                pe.wait_ge(xnT_kept, q + 1)
                pe.wait_ge(h_kept, q + 1)
                for c in range(DC):
                    mm(lqk_ps, wlat[:, c, 0:2 * LAT], xnT[:, c, :], start=(c == 0), stop=(c == DC - 1))
                for c in range(DC):
                    last = mm(lv_ps.rearrange("p b t -> p (b t)"), wlat[:, c, 2 * LAT:3 * LAT], xnT[:, c, :],
                              start=(c == 0), stop=(c == DC - 1))
                last.then_inc(lat_done, 1)

            def values(q):
                pe.wait_ge(lat_kept, 2 * q + 2)
                if not isinstance(q, int) or q >= 1:
                    pe.wait_ge(sub_done, ROWS * q)
                for i in range(2):
                    for b in range(2):
                        last = mm(v_ps[i][:, b, :], lat_v[:, 2 * i + b, :, :].rearrange("p s t -> p (s t)"), wvh[:],
                                  start=True, stop=True)
                    last.then_inc(V_done, 1)

            def queries_keys(q):
                for c in range(DC):
                    last = mm(q_ps[:, c * QT:(c + 1) * QT], wqk_heads[0:LAT, c * 128:(c + 1) * 128],
                              lat_qk[0:LAT, :], start=True, stop=True)
                last.then_inc(Q_done, 1)
                for c in range(DC):
                    last = mm(k_ps[:, c * QT:(c + 1) * QT], wqk_heads[LAT:128, c * 128:(c + 1) * 128],
                              lat_qk[LAT:128, :], start=True, stop=True)
                last.then_inc(K_done, 1)

            def all_scores(q):
                pe.wait_ge(Q_kept, 2 * q + 2)
                pe.wait_ge(K_kept, q + 1)
                pe.wait_ge(V_copied, 2 * q + 2)
                for r in range(ROWS):
                    mm(scores[:, r, :, :].rearrange("p n k -> p (n k)"), ident_bf[:],
                       causal_bf[:].rearrange("p n k -> p (n k)"), start=True, stop=False, skip_group_check=True)
                for n in range(QB * DC):
                    b, c = divmod(n, DC)
                    for r in range(ROWS):
                        strip = slice(32 * r, 32 * r + 32)
                        last = mm(scores[:, r, n, :], Qm[strip, c, b, :, :].rearrange("p a t -> p (a t)"),
                                  Kt[strip, c, b, :], start=False, stop=(n == QB * DC - 1), skip_group_check=True)
                        if n == QB * DC - 1:
                            last.then_inc(S_done, 1)

            def p_transposes(q):
                pe.wait_ge(exp_done, ROWS * (q + 1))
                if not isinstance(q, int) or q >= 1:
                    pe.wait_ge(xn2T_kept, q)
                    pe.wait_ge(s_kept, q)
                for i in range(2):
                    for b in range(2):
                        for j, (s0, n) in enumerate(CH):
                            last = pe.transpose(PT_ps[i][0:n * T, b, j, :],
                                                P[:, 2 * i + b, s0:s0 + n, :].rearrange("p s k -> p (s k)"),
                                                ident[0:HALF, 0:HALF])
                    last.then_inc(PT_done, 1)

            def attend(q):
                pe.wait_ge(V_kept, q + 1)
                if not isinstance(q, int) or q < NQ - 1:
                    pe.wait_ge(hT_kept, q + 2)
                for t in range(2):
                    pe.wait_ge(PT_kept, 2 * q + 2)
                    for j, (s0, n) in enumerate(CH):
                        for a in range(2):
                            for u in range(2):
                                b = 2 * t + u
                                last = mm(y_ps[t][64 * u:64 * u + T, s0:s0 + n, a, :],
                                          PT[0:n * T, b, j, a * T:(a + 1) * T], Vbd[0:n * T, b, s0:s0 + n, a, :],
                                          start=True, stop=True)
                    last.then_inc(y_done, 1)

            def y_transposes(q):
                pe.wait_ge(y_made, 2 * q + 2)
                pe.nop(nofuse=True)
                for t in range(2):
                    for c in range(DC):
                        for u in range(2):
                            last = pe.transpose(yT_ps[u][:, c, t, :], y[64 * u:64 * u + T, t, c * 128:(c + 1) * 128],
                                                ident[64 * u:64 * u + T, 64 * u:64 * u + T])
                last.then_inc(yT_done, 1)

            def project(q):
                pe.wait_ge(yT_kept, 2 * q + 2)
                if isinstance(q, int) and q == 0:
                    pe.wait_ge(proj_in, 16 * 2)
                    pe.wait_ge(ffn_in, 16 * 14)
                for t in range(2):
                    for c in range(DC):
                        last = mm(proj_ps[:, t, :], yT[:, c, 2 * t:2 * t + 2, :].rearrange("p b t -> p (b t)"),
                                  wproj[:, c, :], start=(c == 0), stop=(c == DC - 1))
                last.then_inc(proj_done, 1)

            def xn2_transposes(q):
                for t in range(2):
                    pe.wait_ge(xn2_made, 2 * q + t + 1)
                    for c in range(DC):
                        last = pe.transpose(xn2T_ps[:, c, t * HALF:(t + 1) * HALF], xn2[:, t, c * 128:(c + 1) * 128],
                                            ident[0:HALF, 0:HALF])
                last.then_inc(xn2T_done, 1)

            def ffn_in_product(q):
                pe.wait_ge(xn2T_kept, q + 1)
                if not isinstance(q, int) or q >= 1:
                    pe.wait_ge(o_made, q)
                for c in range(DC):
                    for t in range(2):
                        last = mm(s_ps[64 * t:64 * t + M, :], win[:, c, :], xn2T[:, c, t * HALF:(t + 1) * HALF],
                                  start=(c == 0), stop=(c == DC - 1))
                last.then_inc(s_done, 1)

            def ffn_out_product(q, last_quad=False):
                pe.wait_ge(g_made, q + 1)
                if last_quad:
                    pe.wait_ge(s_kept, q + 1)
                for t in range(2):
                    last = mm(o_ps[t], g[64 * t:64 * t + M, :], wout[64 * t:64 * t + M, :], start=True, stop=True)
                last.then_inc(o_done, 1)

            patches(0)
            token_major(0)
            xn_transposes(0)
            latents(0)
            values(0)
            queries_keys(0)
            all_scores(0)

            def step(i, first=False, last=False):
                if not last:
                    patches(i + 1)
                p_transposes(i)
                if not last:
                    token_major(i + 1)
                attend(i)
                if not last:
                    xn_transposes(i + 1)
                    latents(i + 1)
                y_transposes(i)
                if not last:
                    values(i + 1)
                if not first:
                    ffn_out_product(i - 1)
                if not last:
                    queries_keys(i + 1)
                project(i)
                if not last:
                    all_scores(i + 1)
                xn2_transposes(i)
                ffn_in_product(i)

            steps(pe, step)
            ffn_out_product(NQ - 1, last_quad=True)


def kernel(**inputs):
    import numpy as np
    import concourse.bacc as bacc
    from concourse.bass_utils import run_bass_kernel_spmd as run

    a = {k: np.ascontiguousarray(v) for k, v in inputs.items()}

    def halves(v):
        return v.reshape(DC, 128, -1).transpose(1, 0, 2)

    x = a["x"].reshape(NQ, QB, 3, GRID, PATCH, GRID, PATCH).transpose(0, 2, 4, 6, 1, 3, 5)
    x = x.reshape(NQ, KC, 128, QB * NP).transpose(0, 2, 1, 3).reshape(NQ, 128, KC * QB * NP)
    key, row = np.arange(T), np.arange(HALF) % T
    arrays = {
        "xT": x,
        "wT": a["L0_tok_W"].T.reshape(KC, 128, D).transpose(1, 0, 2),
        "posT": halves(a["L0_tok_pos_embedding"][0, 1:].T),
        "tokb": halves(a["L0_tok_b"][:, None])[:, :, 0],
        "clsT": halves(np.concatenate([a["cls_tok"][0], a["L0_tok_class_token"][0]]).T),
        "pos0T": halves(a["L0_tok_pos_embedding"][0, :1].T)[:, :, 0],
    }
    for name in ("wq_lat", "wk_lat", "wv_lat", "wq_heads", "wk_heads", "wv_heads", "w_proj", "b_proj"):
        arrays[name] = a["L0_attn_" + name]
    for name in ("Win", "bin_", "W1", "b1", "W2", "b2", "Wout", "bout"):
        arrays[name] = a["L0_ffn_" + name]
    arrays["ident_c"] = np.eye(128, dtype=np.float32)
    arrays["causal_c"] = np.where(key[None, :] > row[:, None], np.float32(-1e30), np.float32(0))
    arrays["parity_c"] = (np.arange(128)[:, None] // HD % 2 == np.arange(2)[None, :]).astype(np.float32)
    arrays["block_c"] = (np.arange(S3 * T)[:, None] // T == np.arange(STRIPS)[None, :] % S3).astype(np.float32)

    nc = bacc.Bacc("TRN2", target_bir_lowering=False, num_devices=1)
    feed, aps = {}, []
    for name, v in arrays.items():
        v = np.ascontiguousarray(v)
        feed["in_" + name] = v
        aps.append(nc.dram_tensor("in_" + name, v.shape, F32, kind="ExternalInput").ap())
    out = nc.dram_tensor("out", (IMAGES, T, D), F32, kind="ExternalOutput").ap()
    build(nc, *aps, out)
    r = run(nc, [feed], core_ids=[0])
    return r.results[0]["out"]
```

```python
from contextlib import ExitStack

import concourse.bass as bass
from concourse import mybir

F32 = mybir.dt.float32
BF16 = mybir.dt.bfloat16
ALU = mybir.AluOpType
ACT = mybir.ActivationFunctionType
AX_X = mybir.AxisListType.X

IMAGES = 32
PATCH = 16
GRID = 6
NP = GRID * GRID
T = NP + 2
D = 256
DC = D // 128
KIN = 3 * PATCH * PATCH
KC = KIN // 128
LAT = 64
HEADS = 16
HD = D // HEADS
STRIPS = HEADS // 2
ROWS = 4
M = 64
INNER = 16
ACT_INNER = 10
QB = 4
NQ = IMAGES // QB
QT = QB * T
HALF = QT // 2
S3 = 3
CH = [(0, 3), (3, 3), (6, 2)]
VW = HD + 1
EPS = 1e-5
SCALE = float(HD) ** -0.5


def build(nc, xT, wT, posT, tokb, clsT, pos0T, wq_lat, wk_lat, wv_lat, wq_heads, wk_heads, wv_heads,
          w_proj, b_proj, Win, bin_, W1, b1, W2, b2, Wout, bout, ident_c, causal_c, parity_c, block_c, out):
    with ExitStack() as ctx:
        def sb(name, shape, dt=F32):
            return ctx.enter_context(nc.sbuf_tensor(name, shape, dt))

        def ps(name, shape):
            return ctx.enter_context(nc.psum_tensor(name, shape, F32))

        def sem(name):
            return ctx.enter_context(nc.semaphore(name))

        ident = sb("ident", [128, 128])
        ident_bf = sb("ident_bf", [HALF, HALF], BF16)
        causal = sb("causal", [HALF, T])
        causal_bf = sb("causal_bf", [HALF, QB * DC, T], BF16)
        parity = sb("parity", [128, 2])
        block = sb("block", [S3 * T, STRIPS])
        w_tok = sb("w_tok", [128, KC, D])
        posb = sb("posb", [128, DC, NP])
        tok_bias = sb("tok_bias", [128, DC])
        cls2 = sb("cls2", [128, DC, 2])
        pos0 = sb("pos0", [128, DC])
        wlat = sb("wlat", [128, DC, 3 * LAT])
        wqk_heads = sb("wqk_heads", [128, D])
        wvh = sb("wvh", [LAT, D])
        wproj = sb("wproj", [128, DC, D])
        bproj = sb("bproj", [128, DC])
        win = sb("win", [128, DC, M])
        fbin = sb("fbin", [128, 1])
        fw1 = sb("fw1", [128, INNER])
        fb1 = sb("fb1", [128, INNER])
        fw2 = sb("fw2", [128, INNER])
        fb2 = sb("fb2", [128, 1])
        neg_b1 = sb("neg_b1", [128, INNER])
        w2b1 = sb("w2b1", [128, INNER])
        gconst = sb("gconst", [128, 2])
        wout = sb("wout", [128, D])
        boutb = sb("boutb", [128, DC])
        minus_half = sb("minus_half", [HALF, 2])

        x_sb = sb("x_sb", [128, KC, QB * NP])
        hT = sb("hT", [128, DC, QB, T])
        h_bias = sb("h_bias", [128, NQ, DC, QT])
        st1 = sb("st1", [HALF, 2, 6])
        mv1 = sb("mv1", [HALF, 2, 2])
        ve1 = sb("ve1", [HALF, 2])
        rstd1 = sb("rstd1", [HALF, 2])
        xn = sb("xn", [HALF, 2, D])
        xnT = sb("xnT", [128, DC, QT])
        lat_qk = sb("lat_qk", [128, QT])
        lat_v = sb("lat_v", [LAT, QB, S3, T])
        Qm = sb("Qm", [128, DC, QB, 2, T])
        Kt = sb("Kt", [128, DC, QB, T])
        Vc = sb("Vc", [S3 * T, QB, D])
        Vbd = sb("Vbd", [S3 * T, QB, STRIPS, 2, VW])
        smax = sb("smax", [HALF, ROWS, QB * DC])
        P = sb("P", [HALF, QB, STRIPS, T])
        PT = sb("PT", [S3 * T, QB, len(CH), 2 * T])
        rsum = sb("rsum", [64 + T, 2, STRIPS * 2])
        y = sb("y", [64 + T, 2, D])
        yT = sb("yT", [128, DC, QB, T])
        h2T = sb("h2T", [128, DC, QT])
        h2_bias = sb("h2_bias", [128, NQ, DC, QT])
        st2 = sb("st2", [HALF, 2, 6])
        mv2 = sb("mv2", [HALF, 2, 2])
        ve2 = sb("ve2", [HALF, 2])
        rstd2 = sb("rstd2", [HALF, 2])
        xn2 = sb("xn2", [HALF, 2, D])
        xn2T = sb("xn2T", [128, DC, QT])
        s = sb("s", [128, HALF])
        hid = sb("hid", [128, INNER, HALF])
        hidw = sb("hidw", [128, INNER + 1, HALF])
        g = sb("g", [128, HALF])
        o = sb("o", [128, DC, 2, HALF])

        bank = ps("bank", [128, 8, 512])
        scores = bank[0:HALF, 0:ROWS, 0:QB * DC * T].rearrange("p r (n k) -> p r n k", k=T)
        hT_ps = bank[:, 4, 0:DC * QB * NP].rearrange("p (c n) -> p c n", c=DC)
        xn2T_ps = bank[:, 5, 0:DC * QT].rearrange("p (c n) -> p c n", c=DC)
        o_ps = [bank[:, 6 + t, 0:DC * HALF].rearrange("p (c n) -> p c n", c=DC) for t in range(2)]
        PT_ps = [bank[0:S3 * T, i, 0:2 * len(CH) * 2 * T].rearrange("p (b j n) -> p b j n", b=2, j=len(CH))
                 for i in range(2)]
        h_ps = bank[0:HALF, 2, :].rearrange("p (t d) -> p t d", t=2)
        s_ps = bank[:, 3, 0:HALF]
        y_ps = [bank[0:64 + T, 4 + t, 0:STRIPS * 2 * VW].rearrange("p (s a v) -> p s a v", s=STRIPS, a=2)
                for t in range(2)]
        v_ps = [bank[0:S3 * T, 6 + i, :].rearrange("p (b d) -> p b d", b=2) for i in range(2)]
        yT_ps = [bank[:, u, 0:DC * 2 * T].rearrange("p (c t n) -> p c t n", c=DC, t=2) for u in range(2)]
        xnT_ps = bank[:, 3, 0:DC * QT].rearrange("p (c n) -> p c n", c=DC)
        q_ps = bank[:, 4, 0:DC * QT]
        k_ps = bank[:, 5, 0:DC * QT]
        proj_ps = bank[:, 6, 0:DC * QT].rearrange("p (c n) -> p c n", c=DC)
        lqk_ps = bank[:, 7, 0:QT]
        lv_ps = bank[0:LAT, 7, QT:2 * QT].rearrange("p (b t) -> p b t", b=QB)
        h2_ps = bank[0:HALF, 5, :].rearrange("p (t d) -> p t d", t=2)

        w_tok_in, setup_in, heads_in, proj_in, ffn_in = (
            sem("w_tok_in"), sem("setup_in"), sem("heads_in"), sem("proj_in"), sem("ffn_in"))
        x_in = sem("x_in")
        psum_clear, set_dve, set_pool = sem("psum_clear"), sem("set_dve"), sem("set_pool")
        hT_done, hT_kept = sem("hT_done"), sem("hT_kept")
        h_done = sem("h_done")
        st1_done, mv1_done, ve1_done, rstd1_done, xn_made = (
            sem("st1_done"), sem("mv1_done"), sem("ve1_done"), sem("rstd1_done"), sem("xn_made"))
        xnT_done, xnT_kept = sem("xnT_done"), sem("xnT_kept")
        lat_done, lat_kept = sem("lat_done"), sem("lat_kept")
        V_done, V_copied, V_kept = sem("V_done"), sem("V_copied"), sem("V_kept")
        Q_done, Q_kept = sem("Q_done"), sem("Q_kept")
        K_done, K_kept = sem("K_done"), sem("K_kept")
        S_done, max_done, sub_done, exp_done = sem("S_done"), sem("max_done"), sem("sub_done"), sem("exp_done")
        PT_done, PT_kept = sem("PT_done"), sem("PT_kept")
        y_done, rsum_done, y_made = sem("y_done"), sem("rsum_done"), sem("y_made")
        yT_done, yT_kept = sem("yT_done"), sem("yT_kept")
        proj_done, h2T_made, h2_done = sem("proj_done"), sem("h2T_made"), sem("h2_done")
        h_bias_made, h2_bias_made = sem("h_bias_made"), sem("h2_bias_made")
        st2_done, mv2_done, ve2_done, rstd2_done, xn2_made = (
            sem("st2_done"), sem("mv2_done"), sem("ve2_done"), sem("rstd2_done"), sem("xn2_made"))
        xn2T_done, xn2T_kept = sem("xn2T_done"), sem("xn2T_kept")
        s_done, s_kept = sem("s_done"), sem("s_kept")
        act_hid, dve_hid = sem("act_hid"), sem("dve_hid")
        hidw_made, g_made = sem("hidw_made"), sem("g_made")
        o_done, o_made, o_out = sem("o_done"), sem("o_made"), sem("o_out")
        o_free = sem("o_free")

        x_v = xT.rearrange("q p n -> q p n")
        blk = ctx.enter_context(nc.Block())

        def again(n):
            return not isinstance(n, int) or n >= 1

        def steps(eng, step):
            step(0, lambda n: 0 <= n < NQ)
            step(1, lambda n: 0 <= n < NQ)
            with eng.Fori(2, NQ - 2) as q:
                step(q, lambda n: True)
            step(NQ - 2, lambda n: 0 <= n < NQ)
            step(NQ - 1, lambda n: 0 <= n < NQ)

        @blk.sync
        def _(sp):
            sp.dma_start(x_sb[:].rearrange("p k n -> p (k n)"), x_v[0]).then_inc(x_in, 16)
            sp.dma_start(w_tok[:], wT).then_inc(w_tok_in, 16)
            sp.dma_start(posb[:], posT).then_inc(setup_in, 16)
            sp.dma_start(tok_bias[:], tokb).then_inc(setup_in, 16)
            sp.dma_start(cls2[:], clsT).then_inc(setup_in, 16)
            sp.dma_start(pos0[:], pos0T).then_inc(setup_in, 16)
            sp.dma_start(wproj[:], w_proj.rearrange("(c p) n -> p c n", p=128)).then_inc(proj_in, 16)
            sp.dma_start(win[:], Win.rearrange("(c p) n -> p c n", p=128)).then_inc(proj_in, 16)

            sp.sem_inc(o_free, 1)

            def load(q):
                sp.wait_ge(hT_done, q)
                sp.dma_start(x_sb[:].rearrange("p k n -> p (k n)"),
                             x_v[bass.ds(q, 1)].rearrange("a p n -> (a p) n")).then_inc(x_in, 16)

            def store(q):
                sp.wait_ge(o_made, q + 1)
                sp.dma_start(out[bass.ds(q, 1)].rearrange("a p n -> (a p) n"),
                             o[:].rearrange("p c t n -> p (c t n)")).then_inc(o_out, 16)
                sp.wait_ge(o_out, 16 * (q + 1))
                sp.sem_inc(o_free, 1)

            def step(q, have):
                if have(q + 2):
                    load(q + 2)
                if have(q - 2):
                    store(q - 2)

            load(1)
            steps(sp, step)
            store(NQ - 2)
            store(NQ - 1)

        @blk.gpsimd
        def _(pool):
            for t in range(2):
                rows = slice(64 * t, 64 * t + 64)
                pool.dma_start(wout[rows, :], Wout).then_inc(ffn_in, 16)
                pool.dma_start(fbin[rows, :], bin_.rearrange("(m a) -> m a", a=1)).then_inc(ffn_in, 16)
                pool.dma_start(fw1[rows, :], W1).then_inc(ffn_in, 16)
                pool.dma_start(fb1[rows, :], b1).then_inc(ffn_in, 16)
                pool.dma_start(fw2[rows, :], W2).then_inc(ffn_in, 16)
                pool.dma_start(fb2[rows, :], b2.rearrange("(m a) -> m a", a=1)).then_inc(ffn_in, 16)
            pool.dma_start(bproj[:], b_proj).then_inc(ffn_in, 16)
            pool.dma_start(boutb[:], bout).then_inc(ffn_in, 16)
            pool.memset(minus_half[:], -0.5).then_inc(set_pool, 1)
            pool.memset(Vbd[:], 0.0).then_inc(set_pool, 1)
            pool.wait_ge(set_pool, 2)
            pool.wait_ge(heads_in, 16 * 7)
            for b in range(QB):
                pool.tensor_copy(Vbd[:, b, :, :, HD], block[:].unsqueeze(2).to_broadcast([S3 * T, STRIPS, 2]))\
                    .then_inc(set_pool, 1)
            pool.wait_ge(ffn_in, 16 * 14)

            def rstd(ve, r, ready, done, n):
                pool.wait_ge(ready, n + 1)
                pool.tensor_tensor(r[:], ve[:], minus_half[:], ALU.pow).then_inc(done, 1)

            def weigh_hidden(q, part):
                rows = slice(0, ACT_INNER // 2) if part == 0 else slice(ACT_INNER // 2, INNER)
                if part == 0:
                    pool.wait_ge(act_hid, 2 * q + 1)
                    if again(q):
                        pool.wait_ge(g_made, q)
                else:
                    pool.wait_ge(act_hid, 2 * q + 2)
                    pool.wait_ge(dve_hid, q + 1)
                n = rows.stop - rows.start
                pool.tensor_tensor(hidw[:, rows, :], hid[:, rows, :],
                                   fw2[:, rows].unsqueeze(2).to_broadcast([128, n, HALF]), ALU.mult).then_inc(hidw_made, 1)

            def spread_v(q, first_quad=False):
                if not first_quad:
                    pool.wait_ge(y_done, 2 * q)
                for i in range(2):
                    pool.wait_ge(V_copied, 2 * q + i + 1)
                    for b in (2 * i, 2 * i + 1):
                        last = pool.tensor_tensor(
                            Vbd[:, b, :, :, 0:HD], Vc[:, b, :].rearrange("p (s a d) -> p s a d", s=STRIPS, a=2),
                            block[:].unsqueeze(2).unsqueeze(3).to_broadcast([S3 * T, STRIPS, 2, HD]), ALU.mult)
                last.then_inc(V_kept, 1)

            def add_bproj(q):
                pool.wait_ge(hT_kept, q + 1)
                pool.tensor_tensor(h_bias[:, bass.ds(q, 1), :, :].rearrange("p a c n -> p (a c) n"),
                                   hT[:].rearrange("p c b t -> p c (b t)"),
                                   bproj[:].unsqueeze(2).to_broadcast([128, DC, QT]), ALU.add).then_inc(h_bias_made, 1)

            def add_bout(q):
                pool.wait_ge(h2T_made, q + 1)
                pool.tensor_tensor(h2_bias[:, bass.ds(q, 1), :, :].rearrange("p a c n -> p (a c) n"), h2T[:],
                                   boutb[:].unsqueeze(2).to_broadcast([128, DC, QT]), ALU.add).then_inc(h2_bias_made, 1)

            def norm1(q):
                rstd(ve1, rstd1, ve1_done, rstd1_done, q)
                add_bproj(q)

            norm1(0)
            spread_v(0, first_quad=True)
            norm1(1)

            def step(q, have):
                if have(q + 2):
                    norm1(q + 2)
                if have(q - 1):
                    weigh_hidden(q - 1, 0)
                if have(q + 1):
                    spread_v(q + 1)
                if have(q - 1):
                    weigh_hidden(q - 1, 1)
                rstd(ve2, rstd2, ve2_done, rstd2_done, q)
                add_bout(q)

            steps(pool, step)
            weigh_hidden(NQ - 1, 0)
            weigh_hidden(NQ - 1, 1)

        @blk.scalar
        def _(act):
            act.dma_start(ident[:], ident_c).then_inc(heads_in, 16)
            act.dma_start(causal[:], causal_c).then_inc(heads_in, 16)
            act.dma_start(parity[:], parity_c).then_inc(heads_in, 16)
            act.dma_start(block[:], block_c).then_inc(heads_in, 16)
            for n, w in enumerate((wq_lat, wk_lat, wv_lat)):
                act.dma_start(wlat[:, :, n * LAT:(n + 1) * LAT], w.rearrange("(c p) n -> p c n", p=128)).then_inc(w_tok_in, 16)
            act.dma_start(wqk_heads[0:LAT, :], wq_heads).then_inc(heads_in, 16)
            act.dma_start(wqk_heads[LAT:128, :], wk_heads).then_inc(heads_in, 16)
            act.dma_start(wvh[:], wv_heads).then_inc(heads_in, 16)
            act.wait_ge(heads_in, 16 * 7)
            act.wait_ge(psum_clear, 1)

            def keep_xnT(q):
                act.wait_ge(xnT_done, q + 1)
                act.activation(xnT[:], xnT_ps, ACT.Copy).then_inc(xnT_kept, 1)

            def keep_lat(q):
                act.wait_ge(lat_done, q + 1)
                if again(q):
                    act.wait_ge(K_done, q)
                act.activation(lat_qk[:], lqk_ps, ACT.Copy).then_inc(lat_kept, 1)
                act.activation(lat_v[:], lv_ps.unsqueeze(2).to_broadcast([LAT, QB, S3, T]), ACT.Copy).then_inc(lat_kept, 1)

            def copy_v(q):
                if again(q):
                    act.wait_ge(V_kept, q)
                for i in range(2):
                    act.wait_ge(V_done, 2 * q + i + 1)
                    act.activation(Vc[:, 2 * i:2 * i + 2, :], v_ps[i], ACT.Copy).then_inc(V_copied, 1)

            def keep_qk(q):
                act.wait_ge(Q_done, q + 1)
                if again(q):
                    act.wait_ge(S_done, ROWS * q)
                for a in range(2):
                    act.activation(Qm[:, :, :, a, :].rearrange("p c b t -> p (c b) t"),
                                   q_ps.rearrange("p (n t) -> p n t", t=T), ACT.Copy,
                                   scale=parity[:, a:a + 1]).then_inc(Q_kept, 1)
                act.wait_ge(K_done, q + 1)
                act.activation(Kt[:].rearrange("p c b t -> p (c b t)"), k_ps, ACT.Copy).then_inc(K_kept, 1)

            def exponentials(q):
                for r in range(ROWS):
                    act.wait_ge(sub_done, ROWS * q + r + 1)
                    Pr = P[:].rearrange("p b (c r) k -> p b c r k", r=ROWS)[:, :, :, r, :]
                    act.activation(Pr, Pr, ACT.Exp, scale=SCALE).then_inc(exp_done, 1)

            def keep_PT(q):
                if again(q):
                    act.wait_ge(y_done, 2 * q)
                for i in range(2):
                    act.wait_ge(PT_done, 2 * q + i + 1)
                    act.activation(PT[:, 2 * i:2 * i + 2, :, :], PT_ps[i], ACT.Copy).then_inc(PT_kept, 1)

            def keep_yT(q):
                act.wait_ge(yT_done, q + 1)
                for u in range(2):
                    act.activation(yT[:].rearrange("p c (t u) n -> p c t u n", u=2)[:, :, :, u, :],
                                   yT_ps[u], ACT.Copy).then_inc(yT_kept, 1)

            def keep_xn2T(q):
                act.wait_ge(xn2T_done, q + 1)
                act.activation(xn2T[:], xn2T_ps, ACT.Copy).then_inc(xn2T_kept, 1)

            def hidden(q, part):
                if part == 0:
                    act.wait_ge(s_kept, q + 1)
                    if again(q):
                        act.wait_ge(hidw_made, 2 * q)
                for k in range(ACT_INNER // 2 * part, ACT_INNER // 2 * (part + 1)):
                    last = act.activation(hid[:, k, :], s[:], ACT.Relu, bias=fb1[:, k:k + 1],
                                          scale=fw1[:, k:k + 1])
                last.then_inc(act_hid, 1)

            keep_xnT(0)
            keep_lat(0)
            copy_v(0)
            keep_qk(0)
            keep_xnT(1)
            keep_lat(1)
            act.wait_ge(ffn_in, 16 * 14)

            def step(q, have):
                exponentials(q)
                if have(q - 1):
                    keep_xn2T(q - 1)
                keep_PT(q)
                if have(q - 1):
                    hidden(q - 1, 0)
                if have(q + 1):
                    copy_v(q + 1)
                keep_yT(q)
                if have(q + 2):
                    keep_xnT(q + 2)
                if have(q + 1):
                    keep_qk(q + 1)
                if have(q - 1):
                    hidden(q - 1, 1)
                if have(q + 2):
                    keep_lat(q + 2)

            steps(act, step)
            keep_xn2T(NQ - 1)
            hidden(NQ - 1, 0)
            hidden(NQ - 1, 1)

        @blk.vector
        def _(dve):
            dve.memset(bank[:], 0.0).then_inc(psum_clear, 1)
            dve.memset(rsum[:], 1.0).then_inc(set_dve, 1)
            dve.wait_ge(setup_in, 16 * 4)
            for c in range(DC):
                dve.tensor_scalar(posb[:, c, :], posb[:, c, :], tok_bias[:, c:c + 1], None, ALU.add).then_inc(set_dve, 1)
            for b in range(QB):
                dve.tensor_copy(hT[:, :, b, 0], cls2[:, :, 0]).then_inc(set_dve, 1)
                dve.tensor_tensor(hT[:, :, b, 1], cls2[:, :, 1], pos0[:], ALU.add).then_inc(set_dve, 1)
            dve.wait_ge(heads_in, 16 * 7)
            dve.tensor_copy(ident_bf[:], ident[0:HALF, 0:HALF]).then_inc(set_dve, 1)
            dve.tensor_copy(causal_bf[:], causal[:].unsqueeze(1).to_broadcast([HALF, QB * DC, T])).then_inc(set_dve, 1)
            dve.wait_ge(psum_clear, 1)
            dve.wait_ge(set_dve, 3 + 2 * QB + 2)

            def keep_hT(q):
                dve.wait_ge(hT_done, q + 1)
                if again(q):
                    dve.wait_ge(h_done, q)
                    dve.wait_ge(h_bias_made, q)
                dve.tensor_tensor(hT[:, 0, :, 2:T],
                                  hT_ps[:, 0, :].rearrange("p (b n) -> p b n", b=QB),
                                  posb[:, 0, :].unsqueeze(1).to_broadcast([128, QB, NP]), ALU.add)
                dve.tensor_tensor(hT[:, 1, :, 2:T],
                                  hT_ps[:, 1, :].rearrange("p (b n) -> p b n", b=QB),
                                  posb[:, 1, :].unsqueeze(1).to_broadcast([128, QB, NP]), ALU.add).then_inc(hT_kept, 1)

            def stats(src, st, mv, ve, st_done, mv_done, ve_done, n, ready):
                dve.wait_ge(ready, n + 1)
                for t in range(2):
                    dve.bn_stats(st[:, t, :], src[:, t, :]).then_inc(st_done, 1)
                dve.wait_ge(st_done, 2 * n + 2)
                dve.nop(nofuse=True)
                for t in range(2):
                    dve.bn_aggr(mv[:, t, :], st[:, t, :]).then_inc(mv_done, 1)
                dve.wait_ge(mv_done, 2 * n + 2)
                dve.tensor_scalar(ve[:], mv[:, :, 1], EPS, None, ALU.add).then_inc(ve_done, 1)

            def normalize(src, mv, r, dst, r_done, made, n, free):
                dve.wait_ge(r_done, n + 1)
                if again(n):
                    dve.wait_ge(free, n)
                for t in range(2):
                    dve.tensor_scalar(dst[:, t, :], src[:, t, :], mv[:, t, 0:1], r[:, t:t + 1],
                                      ALU.subtract, ALU.mult).then_inc(made, 1)

            def stats1(q):
                stats(h_ps, st1, mv1, ve1, st1_done, mv1_done, ve1_done, q, h_done)

            def normalize1(q):
                normalize(h_ps, mv1, rstd1, xn, rstd1_done, xn_made, q, xnT_done)

            def stats2(q):
                stats(h2_ps, st2, mv2, ve2, st2_done, mv2_done, ve2_done, q, h2_done)

            def normalize2(q):
                normalize(h2_ps, mv2, rstd2, xn2, rstd2_done, xn2_made, q, xn2T_done)

            def softmax(q):
                if again(q):
                    dve.wait_ge(PT_done, 2 * q)

                def row_max(r):
                    dve.wait_ge(S_done, ROWS * q + r + 1)
                    dve.tensor_reduce(smax[:, r, :], scores[:, r, :, :], AX_X, ALU.max).then_inc(max_done, 1)

                def subtract(r):
                    dve.wait_ge(max_done, ROWS * q + r + 1)
                    dve.tensor_tensor(P[:].rearrange("p b (c r) k -> p b c r k", r=ROWS)[:, :, :, r, :],
                                      scores[:, r, :, :].rearrange("p (b c) k -> p b c k", b=QB),
                                      smax[:, r, :].rearrange("p (b c) -> p b c", b=QB).unsqueeze(3)
                                      .to_broadcast([HALF, QB, DC, T]), ALU.subtract).then_inc(sub_done, 1)

                row_max(0)
                for r in range(1, ROWS):
                    row_max(r)
                    subtract(r - 1)
                subtract(ROWS - 1)

            def weighted_values(q):
                for t in range(2):
                    dve.wait_ge(y_done, 2 * q + t + 1)
                    for u in range(2):
                        rows = slice(64 * u, 64 * u + T)
                        last = dve.reciprocal(rsum[rows, t, :].rearrange("p (s a) -> p s a", a=2), y_ps[t][rows, :, :, HD])
                    last.then_inc(rsum_done, 1)
                if again(q):
                    dve.wait_ge(yT_done, q)
                for t in range(2):
                    dve.wait_ge(rsum_done, 2 * q + t + 1)
                    dve.tensor_tensor(y[:, t, :].rearrange("p (s a d) -> p s a d", s=STRIPS, a=2),
                                      y_ps[t][:, :, :, 0:HD],
                                      rsum[:, t, :].rearrange("p (s a) -> p s a", a=2).unsqueeze(3)
                                      .to_broadcast([64 + T, STRIPS, 2, HD]), ALU.mult).then_inc(y_made, 1)

            def residual2(q):
                dve.wait_ge(proj_done, q + 1)
                dve.wait_ge(h_bias_made, q + 1)
                if again(q):
                    dve.wait_ge(h2_done, q)
                    dve.wait_ge(h2_bias_made, q)
                dve.tensor_tensor(h2T[:], proj_ps, h_bias[:, bass.ds(q, 1), :, :].rearrange("p a c n -> p (a c) n"),
                                  ALU.add).then_inc(h2T_made, 1)

            def keep_s(q):
                dve.wait_ge(s_done, q + 1)
                if again(q):
                    dve.wait_ge(hidw_made, 2 * q)
                dve.tensor_scalar(s[:], s_ps, fbin[:, 0:1], None, ALU.add).then_inc(s_kept, 1)

            def hidden(q):
                dve.wait_ge(s_kept, q + 1)
                for k in range(ACT_INNER, INNER):
                    last = dve.tensor_scalar(hid[:, k, :], s[:], fw1[:, k:k + 1], neg_b1[:, k:k + 1], ALU.mult, ALU.max)
                last.then_inc(dve_hid, 1)

            def sum_hidden(q):
                dve.wait_ge(hidw_made, 2 * q + 2)
                if again(q):
                    dve.wait_ge(o_done, q)
                dve.tensor_reduce(g[:], hidw[:].rearrange("p k n -> p n k"), AX_X, ALU.add).then_inc(g_made, 1)

            def result(q):
                dve.wait_ge(o_done, q + 1)
                dve.wait_ge(h2_bias_made, q + 1)
                dve.wait_ge(o_free, q + 1)
                for t in range(2):
                    last = dve.tensor_tensor(
                        o[:, :, t, :], o_ps[t],
                        h2_bias[:, bass.ds(q, 1), :, t * HALF:(t + 1) * HALF].rearrange("p a c n -> p (a c) n"), ALU.add)
                last.then_inc(o_made, 1)

            def norm1(q):
                keep_hT(q)
                stats1(q)
                normalize1(q)

            norm1(0)
            norm1(1)
            dve.wait_ge(ffn_in, 16 * 14)
            dve.tensor_scalar(neg_b1[:], fb1[:], -1.0, None, ALU.mult).then_inc(set_dve, 1)
            dve.tensor_tensor(w2b1[:], fw2[:], fb1[:], ALU.mult).then_inc(set_dve, 1)
            dve.wait_ge(set_dve, 3 + 2 * QB + 4)
            dve.tensor_reduce(gconst[:, 0:1], w2b1[:, ACT_INNER:], AX_X, ALU.add).then_inc(set_dve, 1)
            dve.wait_ge(set_dve, 3 + 2 * QB + 5)
            dve.tensor_tensor(gconst[:, 1:2], gconst[:, 0:1], fb2[:], ALU.add).then_inc(set_dve, 1)
            dve.wait_ge(set_dve, 3 + 2 * QB + 6)
            dve.tensor_copy(hidw[:, INNER, :], gconst[:, 1:2].to_broadcast([128, HALF])).then_inc(set_dve, 1)
            dve.wait_ge(set_dve, 3 + 2 * QB + 7)

            def step(q, have):
                softmax(q)
                if have(q + 2):
                    keep_hT(q + 2)
                if have(q - 2):
                    result(q - 2)
                if have(q - 1):
                    keep_s(q - 1)
                if have(q + 2):
                    stats1(q + 2)
                weighted_values(q)
                if have(q + 2):
                    normalize1(q + 2)
                if have(q - 1):
                    hidden(q - 1)
                residual2(q)
                stats2(q)
                if have(q - 1):
                    sum_hidden(q - 1)
                normalize2(q)

            steps(dve, step)
            result(NQ - 2)
            keep_s(NQ - 1)
            hidden(NQ - 1)
            sum_hidden(NQ - 1)
            result(NQ - 1)

        @blk.tensor
        def _(pe):
            mm = pe.matmul
            pe.wait_ge(heads_in, 16 * 7)
            pe.wait_ge(w_tok_in, 16 * 4)
            pe.wait_ge(psum_clear, 1)
            pe.wait_ge(set_dve, 3 + 2 * QB + 2)

            def patches(q, first=False):
                pe.wait_ge(x_in, 16 * (q + 1))
                if not first:
                    pe.wait_ge(Q_kept, 2 * (q - 1))
                for c in range(DC):
                    for k in range(KC):
                        last = mm(hT_ps[:, c, :], w_tok[:, k, c * 128:(c + 1) * 128], x_sb[:, k, :],
                                  start=(k == 0), stop=(k == KC - 1))
                last.then_inc(hT_done, 1)

            def token_major(q):
                pe.wait_ge(hT_kept, q + 1)
                if again(q):
                    pe.wait_ge(xn_made, 2 * q)
                for t in range(2):
                    for c in range(DC):
                        last = pe.transpose(h_ps[:, t, c * 128:(c + 1) * 128],
                                            hT[:, c, 2 * t:2 * t + 2, :].rearrange("p b t -> p (b t)"), ident[:])
                last.then_inc(h_done, 1)

            def xn_transposes(q):
                if not isinstance(q, int) or q >= 3:
                    pe.wait_ge(s_kept, q - 2)
                for t in range(2):
                    pe.wait_ge(xn_made, 2 * q + t + 1)
                    for c in range(DC):
                        last = pe.transpose(xnT_ps[:, c, t * HALF:(t + 1) * HALF], xn[:, t, c * 128:(c + 1) * 128],
                                            ident[0:HALF, 0:HALF])
                last.then_inc(xnT_done, 1)

            def latents(q):
                pe.wait_ge(xnT_kept, q + 1)
                if again(q):
                    pe.wait_ge(V_copied, 2 * q)
                for c in range(DC):
                    mm(lqk_ps, wlat[:, c, 0:2 * LAT], xnT[:, c, :], start=(c == 0), stop=(c == DC - 1))
                for c in range(DC):
                    last = mm(lv_ps.rearrange("p b t -> p (b t)"), wlat[:, c, 2 * LAT:3 * LAT], xnT[:, c, :],
                              start=(c == 0), stop=(c == DC - 1))
                last.then_inc(lat_done, 1)

            def values(q):
                pe.wait_ge(lat_kept, 2 * q + 2)
                if not isinstance(q, int) or q >= 3:
                    pe.wait_ge(o_made, q - 2)
                for i in range(2):
                    for b in range(2):
                        last = mm(v_ps[i][:, b, :], lat_v[:, 2 * i + b, :, :].rearrange("p s t -> p (s t)"), wvh[:],
                                  start=True, stop=True)
                    last.then_inc(V_done, 1)

            def queries_keys(q):
                if again(q):
                    pe.wait_ge(y_made, 2 * q)
                for c in range(DC):
                    last = mm(q_ps[:, c * QT:(c + 1) * QT], wqk_heads[0:LAT, c * 128:(c + 1) * 128],
                              lat_qk[0:LAT, :], start=True, stop=True)
                last.then_inc(Q_done, 1)
                for c in range(DC):
                    last = mm(k_ps[:, c * QT:(c + 1) * QT], wqk_heads[LAT:128, c * 128:(c + 1) * 128],
                              lat_qk[LAT:128, :], start=True, stop=True)
                last.then_inc(K_done, 1)

            def all_scores(q):
                pe.wait_ge(Q_kept, 2 * q + 2)
                pe.wait_ge(K_kept, q + 1)
                if again(q):
                    pe.wait_ge(yT_kept, 2 * q)
                if not isinstance(q, int) or q + 1 < NQ:
                    pe.wait_ge(xnT_kept, q + 2)
                else:
                    pe.wait_ge(s_kept, q - 1)
                for r in range(ROWS):
                    mm(scores[:, r, :, :].rearrange("p n k -> p (n k)"), ident_bf[:],
                       causal_bf[:].rearrange("p n k -> p (n k)"), start=True, stop=False, skip_group_check=True)
                for n in range(QB * DC):
                    b, c = divmod(n, DC)
                    for r in range(ROWS):
                        strip = slice(32 * r, 32 * r + 32)
                        last = mm(scores[:, r, n, :], Qm[strip, c, b, :, :].rearrange("p a t -> p (a t)"),
                                  Kt[strip, c, b, :], start=False, stop=(n == QB * DC - 1), skip_group_check=True)
                        if n == QB * DC - 1:
                            last.then_inc(S_done, 1)

            def p_transposes(q):
                pe.wait_ge(exp_done, ROWS * (q + 1))
                for i in range(2):
                    for b in range(2):
                        for j, (s0, n) in enumerate(CH):
                            last = pe.transpose(PT_ps[i][0:n * T, b, j, :],
                                                P[:, 2 * i + b, s0:s0 + n, :].rearrange("p s k -> p (s k)"),
                                                ident[0:HALF, 0:HALF])
                    last.then_inc(PT_done, 1)

            def attend(q, has_h, has_xn2):
                pe.wait_ge(V_kept, q + 1)
                if has_h:
                    pe.wait_ge(hT_kept, q + 3)
                if has_xn2:
                    pe.wait_ge(xn2T_kept, q)
                for t in range(2):
                    pe.wait_ge(PT_kept, 2 * q + 2)
                    for j, (s0, n) in enumerate(CH):
                        for a in range(2):
                            for u in range(2):
                                b = 2 * t + u
                                last = mm(y_ps[t][64 * u:64 * u + T, s0:s0 + n, a, :],
                                          PT[0:n * T, b, j, a * T:(a + 1) * T], Vbd[0:n * T, b, s0:s0 + n, a, :],
                                          start=True, stop=True)
                    last.then_inc(y_done, 1)

            def y_transposes(q):
                pe.wait_ge(y_made, 2 * q + 2)
                pe.nop(nofuse=True)
                for t in range(2):
                    for c in range(DC):
                        for u in range(2):
                            last = pe.transpose(yT_ps[u][:, c, t, :], y[64 * u:64 * u + T, t, c * 128:(c + 1) * 128],
                                                ident[64 * u:64 * u + T, 64 * u:64 * u + T])
                last.then_inc(yT_done, 1)

            def project(q, has_v):
                pe.wait_ge(yT_kept, 2 * q + 2)
                if has_v:
                    pe.wait_ge(V_copied, 2 * q + 4)
                elif isinstance(q, int):
                    pe.wait_ge(o_made, q - 1)
                for c in range(DC):
                    for k in range(DC):
                        last = mm(proj_ps[:, c, :], wproj[:, k, c * 128:(c + 1) * 128],
                                  yT[:, k, :, :].rearrange("p b t -> p (b t)"), start=(k == 0), stop=(k == DC - 1))
                last.then_inc(proj_done, 1)

            def h2_transposes(q, has_k):
                pe.wait_ge(h2T_made, q + 1)
                if has_k:
                    pe.wait_ge(K_kept, q + 2)
                for t in range(2):
                    for c in range(DC):
                        last = pe.transpose(h2_ps[:, t, c * 128:(c + 1) * 128], h2T[:, c, t * HALF:(t + 1) * HALF], ident[:])
                last.then_inc(h2_done, 1)

            def xn2_transposes(q):
                pe.wait_ge(xn2_made, 2 * q + 2)
                for t in range(2):
                    for c in range(DC):
                        last = pe.transpose(xn2T_ps[:, c, t * HALF:(t + 1) * HALF], xn2[:, t, c * 128:(c + 1) * 128],
                                            ident[0:HALF, 0:HALF])
                last.then_inc(xn2T_done, 1)

            def ffn_in_product(q):
                pe.wait_ge(xn2T_kept, q + 1)
                for c in range(DC):
                    for t in range(2):
                        last = mm(s_ps[64 * t:64 * t + M, :], win[:, c, :], xn2T[:, c, t * HALF:(t + 1) * HALF],
                                  start=(c == 0), stop=(c == DC - 1))
                last.then_inc(s_done, 1)

            def ffn_out_product(q, has_lat, has_proj):
                pe.wait_ge(g_made, q + 1)
                if has_proj:
                    pe.wait_ge(h2T_made, q + 2)
                if has_lat:
                    pe.wait_ge(lat_kept, 2 * q + 8)
                for t in range(2):
                    for c in range(DC):
                        last = mm(o_ps[t][:, c, :], wout[64 * t:64 * t + M, c * 128:(c + 1) * 128],
                                  g[64 * t:64 * t + M, :], start=True, stop=True)
                last.then_inc(o_done, 1)

            patches(0, first=True)
            token_major(0)
            xn_transposes(0)
            latents(0)
            pe.wait_ge(hT_kept, 1)
            patches(1, first=True)
            values(0)
            token_major(1)
            pe.wait_ge(hT_kept, 2)
            queries_keys(0)
            xn_transposes(1)
            latents(1)
            all_scores(0)
            pe.wait_ge(proj_in, 16 * 2)
            pe.wait_ge(ffn_in, 16 * 14)

            def step(q, have):
                if have(q + 2):
                    patches(q + 2)
                if have(q - 1):
                    xn2_transposes(q - 1)
                if have(q - 2):
                    ffn_out_product(q - 2, has_lat=have(q + 1), has_proj=True)
                p_transposes(q)
                if have(q + 2):
                    token_major(q + 2)
                if have(q - 1):
                    ffn_in_product(q - 1)
                attend(q, has_h=have(q + 2), has_xn2=have(q - 1))
                if have(q + 1):
                    values(q + 1)
                y_transposes(q)
                if have(q + 2):
                    xn_transposes(q + 2)
                if have(q + 1):
                    queries_keys(q + 1)
                project(q, has_v=have(q + 1))
                if have(q + 2):
                    latents(q + 2)
                h2_transposes(q, has_k=have(q + 1))
                if have(q + 1):
                    all_scores(q + 1)

            steps(pe, step)
            xn2_transposes(NQ - 1)
            ffn_out_product(NQ - 2, has_lat=False, has_proj=True)
            ffn_in_product(NQ - 1)
            pe.wait_ge(o_made, NQ - 1)
            ffn_out_product(NQ - 1, has_lat=False, has_proj=False)


def kernel(**inputs):
    import numpy as np
    import concourse.bacc as bacc
    from concourse.bass_utils import run_bass_kernel_spmd as run

    a = {k: np.ascontiguousarray(v) for k, v in inputs.items()}

    def halves(v):
        return v.reshape(DC, 128, -1).transpose(1, 0, 2)

    x = a["x"].reshape(NQ, QB, 3, GRID, PATCH, GRID, PATCH).transpose(0, 2, 4, 6, 1, 3, 5)
    x = x.reshape(NQ, KC, 128, QB * NP).transpose(0, 2, 1, 3).reshape(NQ, 128, KC * QB * NP)
    key, row = np.arange(T), np.arange(HALF) % T
    arrays = {
        "xT": x,
        "wT": a["L0_tok_W"].T.reshape(KC, 128, D).transpose(1, 0, 2),
        "posT": halves(a["L0_tok_pos_embedding"][0, 1:].T),
        "tokb": halves(a["L0_tok_b"][:, None])[:, :, 0],
        "clsT": halves(np.concatenate([a["cls_tok"][0], a["L0_tok_class_token"][0]]).T),
        "pos0T": halves(a["L0_tok_pos_embedding"][0, :1].T)[:, :, 0],
    }
    for name in ("wq_lat", "wk_lat", "wv_lat", "wq_heads", "wk_heads", "wv_heads", "w_proj", "b_proj"):
        arrays[name] = a["L0_attn_" + name]
    for name in ("Win", "bin_", "W1", "b1", "W2", "b2", "Wout", "bout"):
        arrays[name] = a["L0_ffn_" + name]
    for name in ("b_proj", "bout"):
        arrays[name] = halves(arrays[name][:, None])[:, :, 0]
    arrays["ident_c"] = np.eye(128, dtype=np.float32)
    arrays["causal_c"] = np.where(key[None, :] > row[:, None], np.float32(-1e30), np.float32(0))
    arrays["parity_c"] = (np.arange(128)[:, None] // HD % 2 == np.arange(2)[None, :]).astype(np.float32)
    arrays["block_c"] = (np.arange(S3 * T)[:, None] // T == np.arange(STRIPS)[None, :] % S3).astype(np.float32)

    nc = bacc.Bacc("TRN2", target_bir_lowering=False, num_devices=1)
    feed, aps = {}, []
    for name, v in arrays.items():
        v = np.ascontiguousarray(v)
        feed["in_" + name] = v
        aps.append(nc.dram_tensor("in_" + name, v.shape, F32, kind="ExternalInput").ap())
    out = nc.dram_tensor("out", (NQ, 128, DC * QT), F32, kind="ExternalOutput").ap()
    build(nc, *aps, out)
    r = run(nc, [feed], core_ids=[0])
    o = r.results[0]["out"].reshape(NQ, 128, DC, QB, T).transpose(0, 3, 4, 2, 1)
    return np.ascontiguousarray(o.reshape(IMAGES, T, D))
```

```python
from contextlib import ExitStack

import concourse.bass as bass
from concourse import mybir

F32 = mybir.dt.float32
BF16 = mybir.dt.bfloat16
ALU = mybir.AluOpType
ACT = mybir.ActivationFunctionType
AX_X = mybir.AxisListType.X

IMAGES = 32
PATCH = 16
GRID = 6
NP = GRID * GRID
T = NP + 2
D = 256
DC = D // 128
KIN = 3 * PATCH * PATCH
KC = KIN // 128
LAT = 64
HEADS = 16
HD = D // HEADS
STRIPS = HEADS // 2
ROWS = 4
M = 64
INNER = 16
KH = INNER // 2
QB = 4
NQ = IMAGES // QB
QT = QB * T
HALF = QT // 2
S3 = 3
CH = [(0, 3), (3, 3), (6, 2)]
VW = HD + 1
EPS = 1e-5
SCALE = float(HD) ** -0.5
WARM = 6
SMALL = {"ident": 128, "causal": T, "parity": 2, "side": 2, "block": STRIPS, "tok_bias": DC, "cls2": 2 * DC,
         "pos0": DC, "pos": DC * NP, "bproj": DC, "bout": DC, "fbin": 1, "fw1": KH, "fb1": KH, "fw2": KH, "fb2": 1}
ATT_W = {"wlat": DC * 3 * LAT, "wqk_heads": D, "wv_heads": D}
FFN_W = {"wproj": DC * D, "win": DC * 2 * M, "wout": D}


def columns(fields, name):
    names = list(fields)
    start = sum(fields[n] for n in names[:names.index(name)])
    return slice(start, start + fields[name])


def build(nc, xT, wT, small_in, att_w_in, ffn_w_in, out):
    with ExitStack() as ctx:
        def sb(name, shape, dt=F32):
            return ctx.enter_context(nc.sbuf_tensor(name, shape, dt))

        def ps(name, shape):
            return ctx.enter_context(nc.psum_tensor(name, shape, F32))

        def sem(name):
            return ctx.enter_context(nc.semaphore(name))

        w_tok = sb("w_tok", [128, DC, KC, 128])
        small = sb("small", [128, sum(SMALL.values())])
        att_w = sb("att_w", [128, sum(ATT_W.values())])
        ffn_w = sb("ffn_w", [128, sum(FFN_W.values())])
        ident = small[:, columns(SMALL, "ident")]
        causal = small[0:HALF, columns(SMALL, "causal")]
        parity = small[:, columns(SMALL, "parity")]
        side = small[:, columns(SMALL, "side")]
        block = small[0:S3 * T, columns(SMALL, "block")]
        tok_bias = small[:, columns(SMALL, "tok_bias")]
        cls2 = small[:, columns(SMALL, "cls2")].rearrange("p (c n) -> p c n", c=DC)
        pos0 = small[:, columns(SMALL, "pos0")]
        pos = small[:, columns(SMALL, "pos")].rearrange("p (c n) -> p c n", c=DC)
        bproj = small[:, columns(SMALL, "bproj")]
        boutb = small[:, columns(SMALL, "bout")]
        fbin = small[:, columns(SMALL, "fbin")]
        fw1, fb1 = small[:, columns(SMALL, "fw1")], small[:, columns(SMALL, "fb1")]
        fw2, fb2 = small[:, columns(SMALL, "fw2")], small[:, columns(SMALL, "fb2")]
        wlat = att_w[:, columns(ATT_W, "wlat")].rearrange("p (c n) -> p c n", c=DC)
        wqk_heads = att_w[:, columns(ATT_W, "wqk_heads")]
        wvh = att_w[0:LAT, columns(ATT_W, "wv_heads")]
        wproj = ffn_w[:, columns(FFN_W, "wproj")].rearrange("p (c n) -> p c n", c=DC)
        win = ffn_w[:, columns(FFN_W, "win")].rearrange("p (c n) -> p c n", c=DC)
        wout = ffn_w[:, columns(FFN_W, "wout")]
        ident_bf = sb("ident_bf", [HALF, HALF], BF16)
        causal_bf = sb("causal_bf", [HALF, QB * 2, T], BF16)
        posb = sb("posb", [128, DC, NP])
        minus_half = sb("minus_half", [HALF, 2])
        warm = sb("warm", [1, 1])
        warm_in = sb("warm_in", [128, 512], BF16)

        x_sb = sb("x_sb", [128, KC, QB * NP])
        x1_sb = sb("x1_sb", [128, KC, QB * NP])
        hT = sb("hT", [128, DC, QB, T])
        h_bias = sb("h_bias", [128, NQ, DC, QT])
        st1 = sb("st1", [HALF, 2, 6])
        mv1 = sb("mv1", [HALF, 2, 2])
        ve1 = sb("ve1", [HALF, 2])
        rstd1 = sb("rstd1", [HALF, 2])
        xn = sb("xn", [HALF, 2, D])
        xnT = sb("xnT", [128, DC, QT])
        lat_qk = sb("lat_qk", [128, QT])
        lat_v = sb("lat_v", [LAT, 2, 2, 64])
        Qm = sb("Qm", [128, DC, QB, 2, T])
        Kz = sb("Kz", [128, DC, QB, 2, T])
        V3 = sb("V3", [S3 * T, 2, 2, D])
        Vbd = sb("Vbd", [S3 * T, QB, STRIPS, 2, VW])
        smax = sb("smax", [HALF, ROWS, QB * 2])
        P = sb("P", [HALF, QB, STRIPS, T])
        PT = sb("PT", [S3 * T, QB, len(CH), 2 * T])
        rsum = sb("rsum", [64 + T, 2, STRIPS * 2])
        y = sb("y", [64 + T, 2, D])
        yT = sb("yT", [128, DC, QB, T])
        h2T = sb("h2T", [128, DC, QT])
        h2T_last = sb("h2T_last", [128, DC, QT])
        h2_bias = sb("h2_bias", [128, NQ, DC, QT])
        st2 = sb("st2", [HALF, 2, 6])
        mv2 = sb("mv2", [HALF, 2, 2])
        ve2 = sb("ve2", [HALF, 2])
        rstd2 = sb("rstd2", [HALF, 2])
        xn2 = sb("xn2", [HALF, 2, D])
        xn2T = sb("xn2T", [128, DC, QT])
        s = sb("s", [128, QT])
        hid = sb("hid", [128, KH, QT])
        hidw = sb("hidw", [128, KH + 1, QT])
        hid_last = sb("hid_last", [128, KH, QT])
        hidw_last = sb("hidw_last", [128, KH + 1, QT])
        g = sb("g", [128, QT])
        g_last = sb("g_last", [128, QT])
        o = sb("o", [128, DC, QT])
        o_last = sb("o_last", [128, DC, QT])

        bank = ps("bank", [128, 8, 512])

        def halves_in(n, width=QT):
            return bank[:, n, 0:DC * width].rearrange("p (c n) -> p c n", c=DC)

        def tiles_in(n):
            return bank[0:HALF, n, :].rearrange("p (t d) -> p t d", t=2)

        def PT_in(n):
            return bank[0:S3 * T, n, 0:2 * len(CH) * 2 * T].rearrange("p (b j n) -> p b j n", b=2, j=len(CH))

        def lqk_in(n):
            return bank[:, n, 0:QT]

        def lv_in(n):
            return bank[0:LAT, n, QT:2 * QT]

        def s_in(n):
            return bank[:, n, 0:QT]

        hT1_ps, hT2_ps, h1_ps = halves_in(5, QB * NP), halves_in(0, QB * NP), tiles_in(1)
        scores = bank[0:HALF, 0:ROWS, 0:QB * 2 * T].rearrange("p r (n k) -> p r n k", k=T)
        hT_ps = halves_in(4, QB * NP)
        PT_ps = [PT_in(0), PT_in(1)]
        xn2T_ps = halves_in(5)
        h_ps = tiles_in(2)
        y_ps = [bank[0:64 + T, 4 + t, 0:STRIPS * 2 * VW].rearrange("p (s a v) -> p s a v", s=STRIPS, a=2)
                for t in range(2)]
        s_ps = s_in(3)
        v_ps = bank[0:64 + T, 6, :].rearrange("p (i d) -> p i d", i=2)
        yT_ps = [bank[:, u, 0:DC * 2 * T].rearrange("p (c t n) -> p c t n", c=DC, t=2) for u in range(2)]
        xnT_ps = halves_in(3)
        q_ps, k_ps = halves_in(4), halves_in(5)
        o_ps = halves_in(2)
        proj_ps = halves_in(6)
        h2_ps = tiles_in(5)

        w_tok_in = [sem("w_tok0_in"), sem("w_tok1_in")]
        small_in_sem, att_w_sem, ffn_w_sem = sem("small_in_sem"), sem("att_w_sem"), sem("ffn_w_sem")
        warm_set, warm_done = sem("warm_set"), sem("warm_done")
        x_in, x1_in = sem("x_in"), sem("x1_in")
        x0_in, w0_in = sem("x0_in"), sem("w0_in")
        psum_clear, set_dve, set_pool = sem("psum_clear"), sem("set_dve"), sem("set_pool")
        hT_done, hT_kept = sem("hT_done"), sem("hT_kept")
        h_done = sem("h_done")
        st1_done, mv1_done, ve1_done, rstd1_done, xn_made = (
            sem("st1_done"), sem("mv1_done"), sem("ve1_done"), sem("rstd1_done"), sem("xn_made"))
        xnT_done, xnT_kept = sem("xnT_done"), sem("xnT_kept")
        lat_done, lat_kept = sem("lat_done"), sem("lat_kept")
        V_done, V_copied, V3_in, V_kept = sem("V_done"), sem("V_copied"), sem("V3_in"), sem("V_kept")
        V3_COUNT = 16 * (S3 - 1)
        Q_done, Q_kept = sem("Q_done"), sem("Q_kept")
        K_done, K_kept = sem("K_done"), sem("K_kept")
        S_done, max_done, sub_done, exp_done = sem("S_done"), sem("max_done"), sem("sub_done"), sem("exp_done")
        PT_done, PT_kept = sem("PT_done"), sem("PT_kept")
        y_done, rsum_done, y_made = sem("y_done"), sem("rsum_done"), sem("y_made")
        yT_done, yT_kept = sem("yT_done"), sem("yT_kept")
        proj_done, h2T_made, h2_done = sem("proj_done"), sem("h2T_made"), sem("h2_done")
        h_bias_made, h2_bias_made = sem("h_bias_made"), sem("h2_bias_made")
        st2_done, mv2_done, ve2_done, rstd2_done, xn2_made = (
            sem("st2_done"), sem("mv2_done"), sem("ve2_done"), sem("rstd2_done"), sem("xn2_made"))
        xn2T_done, xn2T_kept = sem("xn2T_done"), sem("xn2T_kept")
        s_done, s_kept = sem("s_done"), sem("s_kept")
        hid_made = sem("hid_made")
        affine_made = sem("affine_made")
        folded = sem("folded")
        hidw_dve_made = sem("hidw_dve_made")
        hidw_made, g_made = sem("hidw_made"), sem("g_made")
        o_done, o_made, o_out = sem("o_done"), sem("o_made"), sem("o_out")

        SET_H = 1 + DC + 2
        SET_DVE = SET_H + 4
        blk = ctx.enter_context(nc.Block())

        def again(n):
            return not isinstance(n, int) or n >= 1

        def steps(eng, step, peeled=0):
            step(0, lambda n: 0 <= n < NQ)
            step(1, lambda n: 0 <= n < NQ)
            with eng.Fori(2, NQ - 2 - peeled) as q:
                step(q, lambda n: True)
            for q in range(NQ - 2 - peeled, NQ - 2):
                step(q, lambda n: 0 <= n < NQ)

        LAST4, LAST3, LAST2, LAST = NQ - 4, NQ - 3, NQ - 2, NQ - 1
        ACT_PARTS = 2 * (LAST3 + 1) + 2

        @blk.sync
        def _(sp):
            x0 = xT[0].rearrange("p (k n) -> p k n", k=KC)
            sp.dma_start(x_sb[:, 0:KC // 2], x0[:, 0:KC // 2]).then_inc(x0_in, 16)
            sp.dma_start(x_sb[:, KC // 2:], x0[:, KC // 2:]).then_inc(x_in, 16)
            sp.dma_start(small[:], small_in).then_inc(small_in_sem, 16)
            sp.dma_start(x1_sb[:].rearrange("p k n -> p (k n)"), xT[1]).then_inc(x1_in, 16)
            sp.dma_start(ffn_w[:], ffn_w_in).then_inc(ffn_w_sem, 16)
            sp.sem_inc(o_out, 16)

            def load(q):
                if isinstance(q, int) and q == 2:
                    sp.wait_ge(hT_done, 2)
                else:
                    sp.wait_ge(hT_done, 2 * q)
                sp.dma_start(x_sb[:].rearrange("p k n -> p (k n)"),
                             xT[bass.ds(q, 1)].rearrange("a p n -> (a p) n")).then_inc(x_in, 16)

            def store(q, src=o):
                sp.wait_ge(o_made, q + 1)
                sp.dma_start(out[bass.ds(q, 1)].rearrange("a p n -> (a p) n"),
                             src[:].rearrange("p c n -> p (c n)")).then_inc(o_out, 16)

            def replicate_v(q):
                sp.wait_ge(V_copied, 2 * q + 2)
                for third in range(1, S3):
                    sp.dma_start(V3[third * T:(third + 1) * T], V3[0:T]).then_inc(V3_in, 16)

            def step(q, have):
                replicate_v(q + 1)
                if have(q + 3):
                    load(q + 3)
                if have(q - 2):
                    store(q - 2)

            load(2)
            replicate_v(0)
            steps(sp, step, peeled=1)
            replicate_v(LAST)
            for q in (LAST4, LAST3, LAST2):
                store(q)
            store(LAST, src=o_last)
            sp.wait_ge(o_out, 16 * (NQ + 1))

        @blk.gpsimd
        def _(pool):
            pool.memset(minus_half[:], -0.5).then_inc(set_pool, 1)
            pool.memset(Vbd[:], 0.0).then_inc(set_pool, 1)
            pool.memset(lat_v[:], 0.0).then_inc(set_pool, 1)
            pool.wait_ge(set_pool, 3)
            pool.wait_ge(small_in_sem, 16)
            for b in range(QB):
                pool.tensor_copy(Vbd[:, b, :, :, HD], block.unsqueeze(2).to_broadcast([S3 * T, STRIPS, 2]))\
                    .then_inc(set_pool, 1)

            def rstd(ve, r, ready, done, n):
                pool.wait_ge(ready, n + 1)
                pool.tensor_tensor(r[:], ve[:], minus_half[:], ALU.pow).then_inc(done, 1)

            def weigh_hidden(q, part, src=hid, dst=hidw, parts=None):
                rows = slice(part * KH // 2, (part + 1) * KH // 2)
                pool.wait_ge(hid_made, 2 * q + part + 1 if parts is None else parts)
                if again(q) and part == 0 and dst is hidw:
                    pool.wait_ge(g_made, q)
                pool.tensor_tensor(dst[:, rows, :], src[:, rows, :],
                                   fw2[:, rows].unsqueeze(2).to_broadcast([128, KH // 2, QT]), ALU.mult).then_inc(hidw_made, 1)

            def fold_hidden(q):
                pool.wait_ge(hidw_made, 2 * q + 2)
                pool.tensor_tensor(hidw[:, KH // 2:KH, :], hidw[:, KH // 2:KH, :], hidw[:, 0:KH // 2, :],
                                   ALU.add).then_inc(folded, 1)

            def spread_v(q):
                if again(q):
                    pool.wait_ge(y_done, 2 * q)
                pool.wait_ge(V3_in, V3_COUNT * (q + 1))
                for b in range(QB):
                    last = pool.tensor_tensor(
                        Vbd[:, b, :, :, 0:HD], V3[:, b // 2, b % 2, :].rearrange("p (s a d) -> p s a d", s=STRIPS, a=2),
                        block.unsqueeze(2).unsqueeze(3).to_broadcast([S3 * T, STRIPS, 2, HD]), ALU.mult)
                last.then_inc(V_kept, 1)

            def add_bproj(q):
                pool.wait_ge(hT_kept, 2 * q + 2)
                pool.tensor_tensor(h_bias[:, bass.ds(q, 1), :, :].rearrange("p a c n -> p (a c) n"),
                                   hT[:].rearrange("p c b t -> p c (b t)"),
                                   bproj.unsqueeze(2).to_broadcast([128, DC, QT]), ALU.add).then_inc(h_bias_made, 1)

            def add_bout(q, src=h2T):
                pool.wait_ge(h2T_made, q + 1)
                pool.tensor_tensor(h2_bias[:, bass.ds(q, 1), :, :].rearrange("p a c n -> p (a c) n"), src[:],
                                   boutb.unsqueeze(2).to_broadcast([128, DC, QT]), ALU.add).then_inc(h2_bias_made, 1)

            def rstd1_of(q):
                rstd(ve1, rstd1, ve1_done, rstd1_done, q)

            for q in range(2):
                add_bproj(q)
                rstd1_of(q)
            spread_v(0)

            def step(q, have):
                if have(q - 2):
                    fold_hidden(q - 2)
                if have(q + 2):
                    rstd1_of(q + 2)
                    add_bproj(q + 2)
                if have(q + 1):
                    spread_v(q + 1)
                if have(q - 1):
                    weigh_hidden(q - 1, 0)
                rstd(ve2, rstd2, ve2_done, rstd2_done, q)
                add_bout(q)
                if have(q - 1):
                    weigh_hidden(q - 1, 1)

            steps(pool, step)
            fold_hidden(LAST4)
            spread_v(LAST)
            weigh_hidden(LAST3, 0)
            weigh_hidden(LAST3, 1)
            rstd(ve2, rstd2, ve2_done, rstd2_done, LAST2)
            fold_hidden(LAST3)
            rstd(ve2, rstd2, ve2_done, rstd2_done, LAST)
            add_bout(LAST2)
            weigh_hidden(LAST2, 0)
            add_bout(LAST, src=h2T_last)
            weigh_hidden(LAST, 0, src=hid_last, dst=hidw_last, parts=ACT_PARTS)

        @blk.scalar
        def _(act):
            act.dma_start(w_tok[:, 0, 0:KC // 2], wT[0][:, 0:KC // 2]).then_inc(w0_in, 16)
            act.dma_start(w_tok[:, 0, KC // 2:], wT[0][:, KC // 2:]).then_inc(w_tok_in[0], 16)
            act.dma_start(w_tok[:, 1], wT[1]).then_inc(w_tok_in[1], 16)
            act.dma_start(att_w[:], att_w_in).then_inc(att_w_sem, 16)
            act.wait_ge(set_pool, 3)
            act.activation(warm[:], minus_half[0:1, 0:1], ACT.Exp).then_inc(warm_done, 1)
            act.wait_ge(small_in_sem, 16)

            def keep_xnT(q):
                act.wait_ge(xnT_done, q + 1)
                act.activation(xnT[:], xnT_ps, ACT.Copy).then_inc(xnT_kept, 1)

            def keep_lat(q, n=7):
                act.wait_ge(lat_done, q + 1)
                if again(q):
                    act.wait_ge(K_done, q)
                    act.wait_ge(V_done, q)
                act.activation(lat_qk[:], lqk_in(n), ACT.Copy).then_inc(lat_kept, 1)
                act.activation(lat_v[:, :, :, 0:T], lv_in(n).rearrange("p (i u t) -> p i u t", i=2, u=2), ACT.Copy).then_inc(lat_kept, 1)

            def copy_v(q):
                if again(q):
                    act.wait_ge(V_kept, q)
                act.wait_ge(V_done, q + 1)
                for u in range(2):
                    act.activation(V3[0:T, :, u, :], v_ps[64 * u:64 * u + T], ACT.Copy).then_inc(V_copied, 1)

            def keep_q(q):
                act.wait_ge(Q_done, q + 1)
                if again(q):
                    act.wait_ge(S_done, ROWS * q)
                for a in range(2):
                    act.activation(Qm[:, :, :, a, :].rearrange("p c b t -> p (c b) t"),
                                   q_ps.rearrange("p c (b t) -> p (c b) t", t=T), ACT.Copy,
                                   scale=parity[:, a:a + 1]).then_inc(Q_kept, 1)

            def keep_k(q):
                act.wait_ge(K_done, q + 1)
                for a in range(2):
                    act.activation(Kz[:, :, :, a, :].rearrange("p c b t -> p (c b) t"),
                                   k_ps.rearrange("p c (b t) -> p (c b) t", t=T), ACT.Copy,
                                   scale=side[:, a:a + 1]).then_inc(K_kept, 1)

            def exponentials(q, r):
                act.wait_ge(sub_done, ROWS * q + r + 1)
                Pr = P[:, :, 2 * r:2 * r + 2, :]
                act.activation(Pr, Pr, ACT.Exp, scale=SCALE).then_inc(exp_done, 1)

            def keep_PT(q, src=PT_ps):
                if again(q):
                    act.wait_ge(y_done, 2 * q)
                for i in range(2):
                    act.wait_ge(PT_done, 2 * q + i + 1)
                    act.activation(PT[:, 2 * i:2 * i + 2, :, :], src[i], ACT.Copy).then_inc(PT_kept, 1)

            def keep_yT(q):
                act.wait_ge(yT_done, q + 1)
                for u in range(2):
                    act.activation(yT[:].rearrange("p c (t u) n -> p c t u n", u=2)[:, :, :, u, :],
                                   yT_ps[u], ACT.Copy).then_inc(yT_kept, 1)

            def keep_xn2T(q, src=xn2T_ps):
                act.wait_ge(xn2T_done, q + 1)
                act.activation(xn2T[:], src, ACT.Copy).then_inc(xn2T_kept, 1)

            def keep_s(q, src=s_ps):
                act.wait_ge(s_done, q + 1)
                if isinstance(q, int) and q == LAST:
                    act.wait_ge(hid_made, ACT_PARTS - 1)
                    act.wait_ge(hidw_dve_made, 1)
                elif again(q):
                    act.wait_ge(hid_made, 2 * q)
                act.activation(s[:], src, ACT.Identity, bias=fbin[:, 0:1]).then_inc(s_kept, 1)

            def hidden(q, part, dst=hid, ks=None):
                start, stop = part * KH // 2, (part + 1) * KH // 2
                if part == 0:
                    act.wait_ge(s_kept, q + 1)
                    if again(q) and dst is hid:
                        act.wait_ge(hidw_made, 2 * q)
                for k in ks or range(start, stop):
                    last = act.activation(dst[:, k, :], s[:], ACT.Relu, bias=fb1[:, k:k + 1], scale=fw1[:, k:k + 1])
                if k == stop - 1:
                    last.then_inc(hid_made, 1)

            keep_xnT(0)
            keep_lat(0)
            keep_q(0)
            keep_xnT(1)
            copy_v(0)
            exponentials(0, 0)
            keep_lat(1, n=5)
            for r in range(1, ROWS):
                exponentials(0, r)

            def step(q, have):
                if not isinstance(q, int) or q > 0:
                    for r in range(ROWS):
                        exponentials(q, r)
                keep_PT(q)
                if have(q - 1):
                    keep_xn2T(q - 1)
                    keep_s(q - 1)
                if have(q + 1):
                    copy_v(q + 1)
                keep_yT(q)
                if have(q + 2):
                    keep_xnT(q + 2)
                if have(q + 1):
                    keep_q(q + 1)
                    keep_k(q + 1)
                if have(q - 1):
                    hidden(q - 1, 0)
                    hidden(q - 1, 1)
                if have(q + 2):
                    keep_lat(q + 2)

            steps(act, step)
            exponentials(LAST2, 0)
            keep_q(LAST)
            exponentials(LAST2, 1)
            exponentials(LAST2, 2)
            exponentials(LAST2, 3)
            copy_v(LAST)
            keep_PT(LAST2, src=[PT_in(4), PT_in(7)])
            keep_xn2T(LAST3)
            for r in range(ROWS):
                exponentials(LAST, r)
            keep_s(LAST3, src=s_in(7))
            keep_PT(LAST, src=[PT_in(3), PT_in(6)])
            keep_yT(LAST2)
            hidden(LAST3, 0)
            hidden(LAST3, 1, ks=range(KH // 2, KH - 2))
            keep_yT(LAST)
            hidden(LAST3, 1, ks=range(KH - 2, KH))
            keep_xn2T(LAST2, src=halves_in(3))
            keep_s(LAST2, src=s_in(7))
            hidden(LAST2, 0)
            keep_xn2T(LAST, src=halves_in(0))
            keep_s(LAST, src=s_in(2))
            hidden(LAST, 0, dst=hid_last)

        @blk.vector
        def _(dve):
            dve.memset(warm_in[:], 0.0).then_inc(warm_set, 1)
            dve.memset(bank[:, 0:2, :], 0.0).then_inc(psum_clear, 1)
            dve.memset(bank[:, 3:7, DC * QT:], 0.0).then_inc(psum_clear, 1)
            dve.memset(rsum[:], 1.0).then_inc(set_dve, 1)
            dve.wait_ge(small_in_sem, 16)
            for c in range(DC):
                dve.tensor_scalar(posb[:, c, :], pos[:, c, :], tok_bias[:, c:c + 1], None, ALU.add).then_inc(set_dve, 1)
            dve.tensor_copy(hT[:, :, :, 0], cls2[:, :, 0].unsqueeze(2).to_broadcast([128, DC, QB])).then_inc(set_dve, 1)
            dve.tensor_tensor(hT[:, :, :, 1], cls2[:, :, 1].unsqueeze(2).to_broadcast([128, DC, QB]),
                              pos0.unsqueeze(2).to_broadcast([128, DC, QB]), ALU.add).then_inc(set_dve, 1)
            dve.wait_ge(set_dve, SET_H)

            def keep_hT(q, src=hT_ps):
                dve.wait_ge(hT_done, 2 * q + 2)
                if again(q):
                    dve.wait_ge(h_done, q)
                    dve.wait_ge(h_bias_made, q)
                for c in range(DC):
                    dve.tensor_tensor(hT[:, c, :, 2:T], src[:, c, :].rearrange("p (b n) -> p b n", b=QB),
                                      posb[:, c, :].unsqueeze(1).to_broadcast([128, QB, NP]), ALU.add).then_inc(hT_kept, 1)

            def stats(src, st, mv, ve, st_done, mv_done, ve_done, n, ready):
                dve.wait_ge(ready, n + 1)
                for t in range(2):
                    dve.bn_stats(st[:, t, :], src[:, t, :]).then_inc(st_done, 1)
                dve.wait_ge(st_done, 2 * n + 2)
                dve.nop(nofuse=True)
                for t in range(2):
                    dve.bn_aggr(mv[:, t, :], st[:, t, :]).then_inc(mv_done, 1)
                dve.wait_ge(mv_done, 2 * n + 2)
                dve.tensor_scalar(ve[:], mv[:, :, 1], EPS, None, ALU.add).then_inc(ve_done, 1)

            def normalize(src, mv, r, dst, r_done, made, n, free):
                dve.wait_ge(r_done, n + 1)
                if again(n):
                    dve.wait_ge(free, n)
                for t in range(2):
                    dve.tensor_scalar(dst[:, t, :], src[:, t, :], mv[:, t, 0:1], r[:, t:t + 1],
                                      ALU.subtract, ALU.mult).then_inc(made, 1)

            def stats1(q, src=h_ps):
                stats(src, st1, mv1, ve1, st1_done, mv1_done, ve1_done, q, h_done)

            def normalize1(q, src=h_ps):
                normalize(src, mv1, rstd1, xn, rstd1_done, xn_made, q, xnT_done)

            def stats2(q, src=h2_ps):
                stats(src, st2, mv2, ve2, st2_done, mv2_done, ve2_done, q, h2_done)

            def normalize2(q, src=h2_ps):
                normalize(src, mv2, rstd2, xn2, rstd2_done, xn2_made, q, xn2T_done)

            def softmax(q):
                if again(q):
                    dve.wait_ge(PT_done, 2 * q)

                def row_max(r):
                    dve.wait_ge(S_done, ROWS * q + r + 1)
                    dve.tensor_reduce(smax[:, r, :], scores[:, r, :, :], AX_X, ALU.max).then_inc(max_done, 1)

                def subtract(r):
                    dve.wait_ge(max_done, ROWS * q + r + 1)
                    dve.tensor_tensor(P[:, :, 2 * r:2 * r + 2, :],
                                      scores[:, r, :, :].rearrange("p (b a) k -> p b a k", b=QB),
                                      smax[:, r, :].rearrange("p (b a) -> p b a", b=QB).unsqueeze(3)
                                      .to_broadcast([HALF, QB, 2, T]), ALU.subtract).then_inc(sub_done, 1)

                row_max(0)
                for r in range(1, ROWS):
                    row_max(r)
                    subtract(r - 1)
                subtract(ROWS - 1)

            def weighted_values(q):
                for t in range(2):
                    dve.wait_ge(y_done, 2 * q + t + 1)
                    for u in range(2):
                        rows = slice(64 * u, 64 * u + T)
                        last = dve.reciprocal(rsum[rows, t, :].rearrange("p (s a) -> p s a", a=2), y_ps[t][rows, :, :, HD])
                    last.then_inc(rsum_done, 1)
                if again(q):
                    dve.wait_ge(yT_done, q)
                for t in range(2):
                    dve.wait_ge(rsum_done, 2 * q + t + 1)
                    dve.tensor_tensor(y[:, t, :].rearrange("p (s a d) -> p s a d", s=STRIPS, a=2),
                                      y_ps[t][:, :, :, 0:HD],
                                      rsum[:, t, :].rearrange("p (s a) -> p s a", a=2).unsqueeze(3)
                                      .to_broadcast([64 + T, STRIPS, 2, HD]), ALU.mult).then_inc(y_made, 1)

            def residual2(q, dst=h2T):
                dve.wait_ge(proj_done, q + 1)
                dve.wait_ge(h_bias_made, q + 1)
                if again(q) and dst is h2T:
                    dve.wait_ge(h2_done, q)
                    dve.wait_ge(h2_bias_made, q)
                dve.tensor_tensor(dst[:], proj_ps, h_bias[:, bass.ds(q, 1), :, :].rearrange("p a c n -> p (a c) n"),
                                  ALU.add).then_inc(h2T_made, 1)

            def sum_hidden(q):
                dve.wait_ge(folded, q + 1)
                if again(q):
                    dve.wait_ge(o_done, q)
                dve.tensor_reduce(g[:], hidw[:, KH // 2:, :].rearrange("p k n -> p n k"), AX_X,
                                  ALU.add).then_inc(g_made, 1)

            def sum_shared(q, n, src, dst):
                dve.wait_ge(hidw_made, 2 * (LAST3 + 1) + n)
                dve.wait_ge(hidw_dve_made, n)
                dve.wait_ge(o_done, LAST2)
                dve.tensor_reduce(dst[:], src[:].rearrange("p k n -> p n k"), AX_X, ALU.add).then_inc(g_made, 1)

            def result(q, src=o_ps, dst=o):
                dve.wait_ge(o_done, q + 1)
                dve.wait_ge(h2_bias_made, q + 1)
                if dst is o:
                    dve.wait_ge(o_out, 16 * (q + 1))
                dve.tensor_tensor(dst[:], src, h2_bias[:, bass.ds(q, 1), :, :].rearrange("p a c n -> p (a c) n"),
                                  ALU.add).then_inc(o_made, 1)

            def keep_k(q, src):
                dve.wait_ge(K_done, q + 1)
                for a in range(2):
                    dve.tensor_scalar(Kz[:, :, :, a, :].rearrange("p c b t -> p (c b) t"),
                                      src.rearrange("p c (b t) -> p (c b) t", t=T), side[:, a:a + 1], None,
                                      ALU.mult).then_inc(K_kept, 1)

            keep_hT(0)
            dve.tensor_copy(ident_bf[:], ident[0:HALF, 0:HALF]).then_inc(set_dve, 1)
            dve.tensor_copy(causal_bf[:], causal.unsqueeze(1).to_broadcast([HALF, QB * 2, T])).then_inc(set_dve, 1)
            for values in (hidw, hidw_last):
                dve.tensor_copy(values[:, KH, :], fb2.to_broadcast([128, QT])).then_inc(set_dve, 1)
            stats1(0)
            keep_hT(1, hT1_ps)
            normalize1(0)
            stats1(1, h1_ps)
            normalize1(1, h1_ps)
            keep_hT(2, hT2_ps)
            keep_k(0, k_ps)

            def step(q, have):
                softmax(q)
                if have(q - 1):
                    normalize2(q - 1)
                    keep_hT(q + 2)
                h = tiles_in(7) if isinstance(q, int) and q == 0 else h_ps
                stats1(q + 2, h)
                weighted_values(q)
                normalize1(q + 2, h)
                if have(q - 2):
                    sum_hidden(q - 2)
                residual2(q)
                if have(q - 2):
                    result(q - 2)
                stats2(q)

            def hidden_and_weigh(q, n, hid, hidw):
                dve.wait_ge(s_kept, q + 1)
                for k in range(KH // 2, KH):
                    dve.tensor_scalar(hid[:, k, :], s[:], fw1[:, k:k + 1], fb1[:, k:k + 1],
                                      ALU.mult, ALU.add).then_inc(affine_made, 1)
                dve.wait_ge(affine_made, n * KH // 2)
                rows = slice(KH // 2, KH)
                dve.scalar_tensor_tensor(hidw[:, rows, :], hid[:, rows, :], 0.0,
                                         fw2[:, rows].unsqueeze(2).to_broadcast([128, KH // 2, QT]),
                                         ALU.max, ALU.mult).then_inc(hidw_dve_made, 1)

            steps(dve, step)
            softmax(LAST2)
            keep_k(LAST, halves_in(7))
            normalize2(LAST3)
            sum_hidden(LAST4)
            softmax(LAST)
            weighted_values(LAST2)
            result(LAST4)
            weighted_values(LAST)
            residual2(LAST2)
            stats2(LAST2, src=tiles_in(2))
            residual2(LAST, dst=h2T_last)
            normalize2(LAST2, src=tiles_in(2))
            stats2(LAST)
            sum_hidden(LAST3)
            normalize2(LAST)
            hidden_and_weigh(LAST2, 1, hid, hidw)
            result(LAST3, src=halves_in(4))
            sum_shared(LAST2, 1, hidw, g)
            hidden_and_weigh(LAST, 2, hid_last, hidw_last)
            sum_shared(LAST, 2, hidw_last, g_last)
            result(LAST2, src=halves_in(1))
            result(LAST, src=halves_in(6), dst=o_last)

        @blk.tensor
        def _(pe):
            mm = pe.matmul

            def keep_busy(n, count, width=256):
                for _ in range(count):
                    mm(bank[:, n, 0:width], warm_in[:, 0:128], warm_in[:, 0:width], start=True, stop=True)

            pe.wait_ge(warm_set, 1)
            keep_busy(7, WARM, width=512)

            def patches(q, c, src=x_sb, dst=hT_ps, ks=range(KC)):
                for k in ks:
                    last = mm(dst[:, c, :], w_tok[:, c, k, :], src[:, k, :], start=(k == 0), stop=(k == KC - 1))
                if KC - 1 in ks:
                    last.then_inc(hT_done, 1)

            def token_major(q, dst=h_ps):
                pe.wait_ge(hT_kept, 2 * q + 2)
                for t in range(2):
                    for c in range(DC):
                        last = pe.transpose(dst[:, t, c * 128:(c + 1) * 128],
                                            hT[:, c, 2 * t:2 * t + 2, :].rearrange("p b t -> p (b t)"), ident[:])
                last.then_inc(h_done, 1)

            def xn_transposes(q):
                for t in range(2):
                    pe.wait_ge(xn_made, 2 * q + t + 1)
                    for c in range(DC):
                        last = pe.transpose(xnT_ps[:, c, t * HALF:(t + 1) * HALF], xn[:, t, c * 128:(c + 1) * 128],
                                            ident[0:HALF, 0:HALF])
                last.then_inc(xnT_done, 1)

            def latents(q, n=7):
                pe.wait_ge(xnT_kept, q + 1)
                for c in range(DC):
                    mm(lqk_in(n), wlat[:, c, 0:2 * LAT], xnT[:, c, :], start=(c == 0), stop=(c == DC - 1))
                for c in range(DC):
                    last = mm(lv_in(n), wlat[:, c, 2 * LAT:3 * LAT], xnT[:, c, :],
                              start=(c == 0), stop=(c == DC - 1))
                last.then_inc(lat_done, 1)

            def values(q):
                pe.wait_ge(lat_kept, 2 * q + 2)
                for i in range(2):
                    last = mm(v_ps[:, i, :], lat_v[:, i, :, :].rearrange("p u t -> p (u t)")[:, 0:64 + T], wvh[:],
                              start=True, stop=True)
                last.then_inc(V_done, 1)

            def queries_keys(q, k_dst=k_ps):
                pe.wait_ge(lat_kept, 2 * q + 2)
                for c in range(DC):
                    last = mm(q_ps[:, c, :], wqk_heads[0:LAT, c * 128:(c + 1) * 128],
                              lat_qk[0:LAT, :], start=True, stop=True)
                last.then_inc(Q_done, 1)
                for c in range(DC):
                    last = mm(k_dst[:, c, :], wqk_heads[LAT:128, c * 128:(c + 1) * 128],
                              lat_qk[LAT:128, :], start=True, stop=True)
                last.then_inc(K_done, 1)

            def all_scores(q):
                pe.wait_ge(Q_kept, 2 * q + 2)
                pe.wait_ge(K_kept, 2 * q + 2)
                for r in range(ROWS):
                    mm(scores[:, r, :, :].rearrange("p n k -> p (n k)"), ident_bf[:],
                       causal_bf[:].rearrange("p n k -> p (n k)"), start=True, stop=False, skip_group_check=True)
                for c in range(DC):
                    for b in range(QB):
                        for half in range(2):
                            r = 2 * c + half
                            rows = slice(64 * half, 64 * half + 64)
                            last = mm(scores[:, r, 2 * b:2 * b + 2, :].rearrange("p a k -> p (a k)"),
                                      Qm[rows, c, b, :, :].rearrange("p a t -> p (a t)"),
                                      Kz[rows, c, b, :, :].rearrange("p a t -> p (a t)"),
                                      start=False, stop=(b == QB - 1), skip_group_check=True)
                            if b == QB - 1:
                                last.then_inc(S_done, 1)

            def p_transposes(q, dst=PT_ps):
                pe.wait_ge(exp_done, ROWS * (q + 1))
                for i in range(2):
                    for b in range(2):
                        for j, (s0, n) in enumerate(CH):
                            last = pe.transpose(dst[i][0:n * T, b, j, :],
                                                P[:, 2 * i + b, s0:s0 + n, :].rearrange("p s k -> p (s k)"),
                                                ident[0:HALF, 0:HALF])
                    last.then_inc(PT_done, 1)

            def attend(q, t):
                if t == 0:
                    pe.wait_ge(V_kept, q + 1)
                pe.wait_ge(PT_kept, 2 * q + t + 1)
                for j, (s0, n) in enumerate(CH):
                    for a in range(2):
                        for u in range(2):
                            b = 2 * t + u
                            last = mm(y_ps[t][64 * u:64 * u + T, s0:s0 + n, a, :],
                                      PT[0:n * T, b, j, a * T:(a + 1) * T], Vbd[0:n * T, b, s0:s0 + n, a, :],
                                      start=True, stop=True)
                last.then_inc(y_done, 1)

            def y_transposes(q):
                for t in range(2):
                    pe.wait_ge(y_made, 2 * q + t + 1)
                    pe.nop(nofuse=True)
                    for c in range(DC):
                        for u in range(2):
                            last = pe.transpose(yT_ps[u][:, c, t, :], y[64 * u:64 * u + T, t, c * 128:(c + 1) * 128],
                                                ident[64 * u:64 * u + T, 64 * u:64 * u + T])
                last.then_inc(yT_done, 1)

            def project(q):
                pe.wait_ge(yT_kept, 2 * q + 2)
                for c in range(DC):
                    for k in range(DC):
                        last = mm(proj_ps[:, c, :], wproj[:, k, c * 128:(c + 1) * 128],
                                  yT[:, k, :, :].rearrange("p b t -> p (b t)"), start=(k == 0), stop=(k == DC - 1))
                last.then_inc(proj_done, 1)

            def h2_transposes(q, dst=h2_ps, src=h2T):
                pe.wait_ge(h2T_made, q + 1)
                for t in range(2):
                    for c in range(DC):
                        last = pe.transpose(dst[:, t, c * 128:(c + 1) * 128], src[:, c, t * HALF:(t + 1) * HALF], ident[:])
                last.then_inc(h2_done, 1)

            def xn2_transposes(q, dst=xn2T_ps):
                pe.wait_ge(xn2_made, 2 * q + 2)
                for t in range(2):
                    for c in range(DC):
                        last = pe.transpose(dst[:, c, t * HALF:(t + 1) * HALF], xn2[:, t, c * 128:(c + 1) * 128],
                                            ident[0:HALF, 0:HALF])
                last.then_inc(xn2T_done, 1)

            def ffn_in_product(q, dst=s_ps):
                pe.wait_ge(xn2T_kept, q + 1)
                for c in range(DC):
                    last = mm(dst, win[:, c, :], xn2T[:, c, :], start=(c == 0), stop=(c == DC - 1))
                last.then_inc(s_done, 1)

            def ffn_out_product(q, dst=o_ps, src=g):
                pe.wait_ge(g_made, q + 1)
                for c in range(DC):
                    last = mm(dst[:, c, :], wout[:, c * 128:(c + 1) * 128], src[:], start=True, stop=True)
                last.then_inc(o_done, 1)

            first_half, second_half = range(KC // 2), range(KC // 2, KC)
            pe.wait_ge(psum_clear, 2)
            pe.wait_ge(x0_in, 16)
            pe.wait_ge(w0_in, 16)
            patches(0, 0, ks=first_half)
            pe.wait_ge(x_in, 16)
            pe.wait_ge(w_tok_in[0], 16)
            patches(0, 0, ks=second_half)
            pe.wait_ge(w_tok_in[1], 16)
            patches(0, 1)
            pe.wait_ge(x1_in, 16)
            patches(1, 0, x1_sb, hT1_ps)
            token_major(0)
            patches(1, 1, x1_sb, hT1_ps)
            pe.wait_ge(x_in, 32)
            patches(2, 0, dst=hT2_ps, ks=first_half)
            token_major(1, dst=h1_ps)
            xn_transposes(0)
            patches(2, 0, dst=hT2_ps, ks=second_half)
            pe.wait_ge(att_w_sem, 16)
            latents(0)
            patches(2, 1, dst=hT2_ps)
            queries_keys(0)
            xn_transposes(1)
            values(0)
            pe.wait_ge(set_dve, SET_DVE)
            pe.wait_ge(hT_kept, 6)
            pe.wait_ge(xnT_kept, 2)
            all_scores(0)
            latents(1, n=5)
            token_major(2, dst=tiles_in(7))
            keep_busy(4, 3)
            pe.wait_ge(V_copied, 2)
            values(1)
            pe.wait_ge(ffn_w_sem, 16)

            def step(q, have):
                if not isinstance(q, int) or q > 0:
                    pe.wait_ge(x_in, 16 * (q + 2))
                    for c in range(DC):
                        patches(q + 2, c)
                p_transposes(q)
                if have(q - 1):
                    xn2_transposes(q - 1)
                if not isinstance(q, int) or q > 0:
                    token_major(q + 2)
                if isinstance(q, int) and q == 0:
                    keep_busy(3, 4)
                attend(q, 0)
                if have(q - 1):
                    pe.wait_ge(xn2T_kept, q)
                attend(q, 1)
                if have(q - 1):
                    ffn_in_product(q - 1)
                if isinstance(q, int) and q == 0:
                    keep_busy(0, 8)
                else:
                    values(q + 1)
                y_transposes(q)
                queries_keys(q + 1)
                if have(q - 1):
                    pe.wait_ge(s_kept, q)
                xn_transposes(q + 2)
                pe.wait_ge(V_copied, 2 * q + 4)
                project(q)
                if have(q - 2):
                    ffn_out_product(q - 2)
                latents(q + 2)
                pe.wait_ge(K_kept, 2 * q + 4)
                h2_transposes(q)
                if have(q - 2):
                    pe.wait_ge(o_made, q - 1)
                all_scores(q + 1)

            steps(pe, step)
            queries_keys(LAST, k_dst=halves_in(7))
            values(LAST)
            pe.wait_ge(sub_done, ROWS * LAST2 + 2)
            keep_busy(1, 8)
            pe.wait_ge(Q_kept, 2 * NQ)
            pe.wait_ge(K_kept, 2 * NQ)
            p_transposes(LAST2, dst=[PT_in(4), PT_in(7)])
            xn2_transposes(LAST3)
            all_scores(LAST)
            attend(LAST2, 0)
            pe.wait_ge(xn2T_kept, LAST3 + 1)
            attend(LAST2, 1)
            ffn_in_product(LAST3, dst=s_in(7))
            pe.wait_ge(sub_done, ROWS * LAST + 3)
            ffn_out_product(LAST4)
            pe.wait_ge(V_copied, 2 * NQ)
            p_transposes(LAST, dst=[PT_in(3), PT_in(6)])
            y_transposes(LAST2)
            attend(LAST, 0)
            attend(LAST, 1)
            project(LAST2)
            y_transposes(LAST)
            pe.wait_ge(o_made, LAST4 + 1)
            h2_transposes(LAST2, dst=tiles_in(2))
            project(LAST)
            keep_busy(4, 5)
            h2_transposes(LAST, src=h2T_last)
            keep_busy(4, 7)
            xn2_transposes(LAST2, dst=halves_in(3))
            keep_busy(4, 6)
            pe.wait_ge(s_kept, LAST3 + 1)
            ffn_in_product(LAST2, dst=s_in(7))
            keep_busy(4, 4)
            ffn_out_product(LAST3, dst=halves_in(4))
            keep_busy(3, 3)
            xn2_transposes(LAST, dst=halves_in(0))
            keep_busy(3, 8)
            ffn_in_product(LAST, dst=s_in(2))
            keep_busy(3, 12)
            ffn_out_product(LAST2, dst=halves_in(1))
            keep_busy(3, 20)
            ffn_out_product(LAST, dst=halves_in(6), src=g_last)


def kernel(**inputs):
    import numpy as np
    import concourse.bacc as bacc
    from concourse.bass_utils import run_bass_kernel_spmd as run

    a = {k: np.ascontiguousarray(v) for k, v in inputs.items()}

    def halves(v):
        return v.reshape(DC, 128, -1).transpose(1, 0, 2)

    x = a["x"].reshape(NQ, QB, 3, GRID, PATCH, GRID, PATCH).transpose(0, 2, 4, 6, 1, 3, 5)
    x = x.reshape(NQ, KC, 128, QB * NP).transpose(0, 2, 1, 3).reshape(NQ, 128, KC * QB * NP)
    t, f = "L0_attn_", "L0_ffn_"

    def pack(fields, parts):
        box = np.zeros((128, sum(fields.values())), np.float32)
        for name in fields:
            v = parts[name].reshape(parts[name].shape[0], -1)
            box[:v.shape[0], columns(fields, name)] = v
        return box

    def inner(v):
        return v.reshape(M, 2, KH).transpose(1, 0, 2).reshape(128, KH)

    key, row, part = np.arange(T), np.arange(HALF) % T, np.arange(128)[:, None]
    small = {
        "ident": np.eye(128, dtype=np.float32),
        "causal": np.where(key[None, :] > row[:, None], np.float32(-1e30), np.float32(0)),
        "parity": part // HD % 2 == np.arange(2),
        "side": part // (2 * HD) % 2 == np.arange(2),
        "block": part[:S3 * T] // T == np.arange(STRIPS) % S3,
        "tok_bias": halves(a["L0_tok_b"][:, None]),
        "cls2": halves(np.concatenate([a["cls_tok"][0], a["L0_tok_class_token"][0]]).T),
        "pos0": halves(a["L0_tok_pos_embedding"][0, :1].T),
        "pos": halves(a["L0_tok_pos_embedding"][0, 1:].T),
        "bproj": halves(a[t + "b_proj"][:, None]),
        "bout": halves(a[f + "bout"][:, None]),
        "fbin": np.concatenate([a[f + "bin_"]] * 2)[:, None],
        "fw1": inner(a[f + "W1"]),
        "fb1": inner(a[f + "b1"]),
        "fw2": inner(a[f + "W2"]),
        "fb2": a[f + "b2"][:, None],
    }
    att = {
        "wlat": np.concatenate([halves(a[t + n]) for n in ("wq_lat", "wk_lat", "wv_lat")], axis=2),
        "wqk_heads": np.concatenate([a[t + "wq_heads"], a[t + "wk_heads"]]),
        "wv_heads": a[t + "wv_heads"],
    }
    ffn = {
        "wproj": halves(a[t + "w_proj"]),
        "win": np.concatenate([halves(a[f + "Win"])] * 2, axis=2),
        "wout": np.concatenate([a[f + "Wout"]] * 2),
    }
    arrays = {
        "xT": x,
        "wT": a["L0_tok_W"].T.reshape(KC, 128, DC, 128).transpose(2, 1, 0, 3),
        "small": pack(SMALL, small),
        "att_w": pack(ATT_W, att),
        "ffn_w": pack(FFN_W, ffn),
    }

    nc = bacc.Bacc("TRN2", target_bir_lowering=False, num_devices=1)
    feed, aps = {}, []
    for name, v in arrays.items():
        v = np.ascontiguousarray(v)
        feed["in_" + name] = v
        aps.append(nc.dram_tensor("in_" + name, v.shape, F32, kind="ExternalInput").ap())
    out = nc.dram_tensor("out", (NQ, 128, DC * QT), F32, kind="ExternalOutput").ap()
    build(nc, *aps, out)
    r = run(nc, [feed], core_ids=[0])
    o = r.results[0]["out"].reshape(NQ, 128, DC, QB, T).transpose(0, 3, 4, 2, 1)
    return np.ascontiguousarray(o.reshape(IMAGES, T, D))
```
